# Optimizing a Trainium2 kernel written in Bass

```python
import numpy as np
import jax
import jax.numpy as jnp

def _softmax(x, axis=-1):
    return jax.nn.softmax(x, axis=axis)

def _gelu(x):
    return jax.nn.gelu(x, approximate=True)

def _silu(x):
    return jax.nn.silu(x)

def _sigmoid(x):
    return jax.nn.sigmoid(x)

def _layernorm(x, axis=-1, eps=1e-05):
    m = jnp.mean(x, axis=axis, keepdims=True)
    v = jnp.var(x, axis=axis, keepdims=True)
    return (x - m) / jnp.sqrt(v + eps)

def _scatter_add(tgt, idx, src, axis=0):
    return tgt.at[idx].add(src)

def _segment_sum(src, seg, n):
    return jax.ops.segment_sum(src, seg, n)
kernel_name = 'mk_seq_preln_d1_jaxref_r8_1e9da8'

def setup_inputs(seed: int=0):
    np.random.seed(seed)
    _w = jnp.asarray

    def _L0_attn_setup():
        import jax, jax.numpy as jnp
        import numpy as np
        B, S, D, H = (2, 256, 128, 16)
        DEPTH = D // H
        EPS = 1e-06

        def _split_heads(t):
            b, s, _ = t.shape
            return t.reshape(b, s, H, DEPTH).transpose(0, 2, 1, 3)
        key = jax.random.key(seed)
        ks = jax.random.split(key, 6)
        glorot = lambda k: jax.random.uniform(k, (D, D), jnp.float32, -1.0, 1.0) * np.sqrt(6.0 / (D + D))
        return {'x': jax.random.normal(ks[0], (B, S, D), jnp.float32), 'Wq': glorot(ks[1]), 'bq': jnp.zeros((D,), jnp.float32), 'Wk': glorot(ks[2]), 'bk': jnp.zeros((D,), jnp.float32), 'Wv': glorot(ks[3]), 'bv': jnp.zeros((D,), jnp.float32), 'Wo': glorot(ks[4]), 'bo': jnp.zeros((D,), jnp.float32), 'gamma': jnp.ones((D,), jnp.float32), 'beta': jnp.zeros((D,), jnp.float32)}
    _L0_attn_in = _L0_attn_setup()

    def _L0_ffn_setup():
        import jax, jax.numpy as jnp
        import numpy as np
        CAPACITY_RATIO = 0.75
        key = jax.random.key(seed)
        k1, k2, k3 = jax.random.split(key, 3)
        B, L, D = (4, 1024, 128)
        x = jax.random.normal(k1, (B, L, D), dtype=jnp.float32)
        w_router = jax.random.normal(k2, (D,), dtype=jnp.float32) * 0.02
        w_block = jax.random.normal(k3, (D, D), dtype=jnp.float32) * 0.02
        return {'x': x, 'w_router': w_router, 'w_block': w_block}
    _L0_ffn_in = _L0_ffn_setup()
    _d = {'L0_attn_x': _L0_attn_in['x'], 'L0_attn_Wq': _L0_attn_in['Wq'], 'L0_attn_bq': _L0_attn_in['bq'], 'L0_attn_Wk': _L0_attn_in['Wk'], 'L0_attn_bk': _L0_attn_in['bk'], 'L0_attn_Wv': _L0_attn_in['Wv'], 'L0_attn_bv': _L0_attn_in['bv'], 'L0_attn_Wo': _L0_attn_in['Wo'], 'L0_attn_bo': _L0_attn_in['bo'], 'L0_attn_gamma': _L0_attn_in['gamma'], 'L0_attn_beta': _L0_attn_in['beta'], 'L0_ffn_w_router': _L0_ffn_in['w_router'], 'L0_ffn_w_block': _L0_ffn_in['w_block']}
    _x0 = _d['L0_attn_x']
    _d['L0_attn_x'] = jax.random.normal(jax.random.fold_in(jax.random.key(seed), 1), (4, 1024, 128), dtype=_x0.dtype)
    del _x0
    return _d

def reference(L0_attn_x, L0_attn_Wq, L0_attn_bq, L0_attn_Wk, L0_attn_bk, L0_attn_Wv, L0_attn_bv, L0_attn_Wo, L0_attn_bo, L0_attn_gamma, L0_attn_beta, L0_ffn_w_router, L0_ffn_w_block):

    def _L0_attn_ref(x, Wq, bq, Wk, bk, Wv, bv, Wo, bo, gamma, beta):
        import jax, jax.numpy as jnp
        import numpy as np
        B, S, D, H = (2, 256, 128, 16)
        DEPTH = D // H
        EPS = 1e-06

        def _split_heads(t):
            b, s, _ = t.shape
            return t.reshape(b, s, H, DEPTH).transpose(0, 2, 1, 3)
        b, s, d = x.shape
        q = _split_heads(x @ Wq + bq)
        k = _split_heads(x @ Wk + bk)
        v = _split_heads(x @ Wv + bv)
        q = jax.nn.elu(q) + 1.0
        k = jax.nn.elu(k) + 1.0
        k = k / jnp.sqrt(jnp.sum(k * k, axis=-1, keepdims=True) + EPS)
        scores = jnp.einsum('bhqd,bhkd->bhqk', q, k)
        attn = jnp.einsum('bhqk,bhkd->bhqd', scores, v)
        attn = attn.transpose(0, 2, 1, 3).reshape(b, s, d)
        out = attn @ Wo + bo
        y = x + out
        mu = jnp.mean(y, axis=-1, keepdims=True)
        var = jnp.mean(jnp.square(y - mu), axis=-1, keepdims=True)
        return (y - mu) / jnp.sqrt(var + EPS) * gamma + beta

    def _L0_ffn_ref(x, w_router, w_block):
        import jax, jax.numpy as jnp
        import numpy as np
        CAPACITY_RATIO = 0.75
        B, L, D = x.shape
        k = max(1, int(L * CAPACITY_RATIO))
        scores = jnp.einsum('bld,d->bl', x, w_router)
        _, top_idx = jax.lax.top_k(scores, k)
        selected = jnp.take_along_axis(x, top_idx[:, :, None], axis=1)
        processed = jax.nn.gelu(jnp.einsum('bkd,de->bke', selected, w_block))
        batch_idx = jnp.arange(B)[:, None]
        out = x.at[batch_idx, top_idx].set(processed)
        return out
    x = L0_attn_x
    x = x + _L0_attn_ref(_layernorm(x, axis=-1), L0_attn_Wq, L0_attn_bq, L0_attn_Wk, L0_attn_bk, L0_attn_Wv, L0_attn_bv, L0_attn_Wo, L0_attn_bo, L0_attn_gamma, L0_attn_beta)
    x = x + _L0_ffn_ref(_layernorm(x, axis=-1), L0_ffn_w_router, L0_ffn_w_block)
    return x

_drawn_inputs = setup_inputs


def setup_inputs(seed=0):
    import zlib

    import numpy as np

    out = dict(_drawn_inputs(seed))
    spreads = {'L0_attn_bq': (0.0, 0.1),
     'L0_attn_bk': (0.0, 0.1),
     'L0_attn_bv': (0.0, 0.1),
     'L0_attn_bo': (0.0, 0.1),
     'L0_attn_gamma': (1.0, 0.2),
     'L0_attn_beta': (0.0, 0.1)}
    factors = {}
    for name, (base, spread) in spreads.items():
        noise = np.random.default_rng([zlib.crc32(name.encode()), seed]).standard_normal(out[name].shape)
        drawn = base * np.exp(spread * noise) if base else spread * noise
        out[name] = jnp.asarray(drawn.astype(out[name].dtype))
    for name, factor in factors.items():
        out[name] = (out[name] * factor).astype(out[name].dtype)
    return out
```

```python
from contextlib import ExitStack

import concourse.bass as bass
from concourse import mybir

ALU = mybir.AluOpType
ACT = mybir.ActivationFunctionType
F32 = mybir.dt.float32
BF16 = mybir.dt.bfloat16
I32 = mybir.dt.int32

P = 128
HEADS, DEPTH = 16, 8
LN_EPS = 1e-5
ATTN_EPS = 1e-6
CAPACITY = 0.75
TH = 4


def preln_linear_attention_mod_ffn(nc, x, wq, bq, wk, bk, wv, bv, wo, bo, gamma, beta, w_router, w_block, out):
    B, L, D = x.shape
    assert D == P and HEADS * DEPTH == D and L % (2 * TH * P) == 0
    T = L // P
    U = B * T // TH
    HW = TH * P
    KEEP = max(1, int(L * CAPACITY))
    assert T == 2 * TH

    x_v = x.rearrange("b (t p) d -> b p t d", p=P)
    out_v = out.rearrange("b (t p) d -> b p t d", p=P)

    with ExitStack() as ctx:
        def sb(name, shape, dt=F32):
            return ctx.enter_context(nc.sbuf_tensor(name, shape, dt))

        def sem(name):
            return ctx.enter_context(nc.semaphore(name))

        x_sb = sb("x_sb", [P, B * T, D])
        xb_sb = sb("xb_sb", [P, B * T, D])
        norm_sb = sb("norm_sb", [P, B * T, D])
        hT = sb("hT", [P, U, HW])
        qT = sb("qT", [P, U, HW])
        exp_q = sb("exp_q", [P, 2, HW])
        exp_k = sb("exp_k", [P, 2, HW])
        k_sb = sb("k_sb", [P, 4, TH, D])
        k2_sb = sb("k2_sb", [P, 2, TH * HEADS, DEPTH])
        k_add4 = sb("k_add4", [P, 2, TH * HEADS, 4])
        k_add2 = sb("k_add2", [P, 2, TH * HEADS, 2])
        k_ssq = sb("k_ssq", [P, 2, TH * HEADS])
        k_rnorm = sb("k_rnorm", [P, 2, TH * HEADS])
        v_sb = sb("v_sb", [P, 4, TH, D])
        vk_sb = sb("vk_sb", [P, 2, P])
        M_sb = sb("M_sb", [P, B, P])
        yn_sb = sb("yn_sb", [P, 2, TH, D])
        h2T = sb("h2T", [P, 2, HW])
        g_sb = sb("g_sb", [P, B * T, D])
        s_col = sb("s_col", [P, B * T])
        s_row = sb("s_row", [P, 2, T * P])
        beats = sb("beats", [P, 2, T, T * P], BF16)
        ties = sb("ties", [P, 2, T, P], BF16)
        rank_sb = sb("rank_sb", [P, 2, T])
        dropped = sb("dropped", [P, 2, T], I32)
        bn1 = sb("bn1", [P, B * T // 2, 6])
        bny = sb("bny", [P, B * T // 2, 6])
        bn3 = sb("bn3", [P, B * T // 2, 6])
        var1 = sb("var1", [P, B * T])
        vary = sb("vary", [P, B * T])
        var3 = sb("var3", [P, B * T])
        r1 = sb("r1", [P, B * T])
        ry = sb("ry", [P, B * T])
        r3 = sb("r3", [P, B * T])
        neg_ry = sb("neg_ry", [P, B * T])
        shift_y = sb("shift_y", [P, B * T])
        ident = sb("ident", [P, P])
        lower = sb("lower", [P, P])
        head_mask = sb("head_mask", [P, P])
        minus_half = sb("minus_half", [P, TH * HEADS])
        minus_one = sb("minus_one", [P, T])
        minus1 = sb("minus1", [P, 1])
        ones_col = sb("ones_col", [P, 1], BF16)
        ones3 = sb("ones3", [3, HW], BF16)
        wq_sb = sb("wq_sb", [P, P])
        wkv_sb = sb("wkv_sb", [P, 2 * P])
        wo_sb = sb("wo_sb", [P, P])
        wz_sb = sb("wz_sb", [P, P + 1])
        gamma_sb = sb("gamma_sb", [P, P])
        beta_sb = sb("beta_sb", [P, P])
        bias_f = sb("bias_f", [3, 4 * P])
        bias_hi = sb("bias_hi", [3, 4 * P], BF16)
        bias_r1 = sb("bias_r1", [3, 4 * P])
        bias_mid = sb("bias_mid", [3, 4 * P], BF16)
        bias_r2 = sb("bias_r2", [3, 4 * P])
        bias_lo = sb("bias_lo", [3, 4 * P], BF16)
        bias_m = sb("bias_m", [3, 3, 4 * P])
        bias3 = sb("bias3", [3, 4 * P], BF16)

        bank = ctx.enter_context(nc.psum_tensor("bank", [P, 8, HW], F32))
        T_BANKS = (0, 1)
        Q_BANKS = (2, 3)
        Y_BANKS = (2, 3, 6, 7)

        def kv_ps(u):
            a = 4 + 2 * (u % 2)
            return bank[:, a:a + 2, :].rearrange("p a (t c) -> p (a t) c", c=2 * P)

        def z_ps():
            return bank[:, 4:6, 0:2 * (P + 1)].rearrange("p a (t c) -> p a t c", c=P + 1)

        x_in = [sem(f"x_in{b}") for b in range(2 * B)]
        wq_in, wkv_in, wo_in, wz_in = sem("wq_in"), sem("wkv_in"), sem("wo_in"), sem("wz_in")
        bias_in, gb_in = sem("bias_in"), sem("gb_in")
        out_stored = sem("out_stored")
        pool_chain = sem("pool_chain")
        dve_chain = sem("dve_chain")
        ident_set, lower_set, mask_set = sem("ident_set"), sem("lower_set"), sem("mask_set")
        dve_const, bias_set = sem("dve_const"), sem("bias_set")
        bn1_done, r1_done, h_done = sem("bn1_done"), sem("r1_done"), sem("h_done")
        t_full, t_free = sem("t_full"), sem("t_free")
        vk_full, vk_done = sem("vk_full"), sem("vk_done")
        hT_done, q_full, expq_done, q_done = sem("hT_done"), sem("q_full"), sem("expq_done"), sem("q_done")
        kv_full, expk_done, k_done, k2_done = sem("kv_full"), sem("expk_done"), sem("k_done"), sem("k2_done")
        rnorm_done, v_done, M_done = sem("rnorm_done"), sem("v_done"), sem("M_done")
        xb_done = sem("xb_done")
        y_full, bny_done, ry_done, yn_done = sem("y_full"), sem("bny_done"), sem("ry_done"), sem("yn_done")
        x1_done, bn3_done, r3_done, h2_done = sem("x1_done"), sem("bn3_done"), sem("r3_done"), sem("h2_done")
        h2T_done, z_full, gelu_done, s_col_done = sem("h2T_done"), sem("z_full"), sem("gelu_done"), sem("s_col_done")
        beats_done = sem("beats_done")
        dropped_done, merged, final_done = sem("dropped_done"), sem("merged"), sem("final_done")

        RANK_LAG = 6
        t_uses = []
        for b in range(B):
            t_uses += [("h", 2 * b), ("h", 2 * b + 1)]
            if b:
                t_uses += [("M", b - 1)]
        t_uses += [("M", B - 1)]
        for s in range(U + RANK_LAG):
            if 2 <= s < U + 2:
                t_uses += [("h2", s - 2)]
            if 3 <= s < U + 3:
                t_uses += [("s", s - 3)]
            if s >= RANK_LAG and (s - RANK_LAG) % 2 == 0:
                t_uses += [("r", (s - RANK_LAG) // 2)]
        t_at = {use: n for n, use in enumerate(t_uses)}

        def t_bank(use):
            return bank[:, T_BANKS[t_at[use] % 2], :]

        def stats(bn, a, n):
            v = bn[:, :, :].rearrange("p g (e s) -> p (g e) s", s=3)
            return v[:, a:a + n, 1], v[:, a:a + n, 2]

        def pairs(ap, g):
            return ap[:, 2 * g:2 * g + 2, :].rearrange("p t d -> p d t")

        block = ctx.enter_context(nc.Block())

        @block.sync
        def _(sp):
            for u in range(2 * B):
                b, a = u // 2, TH * (u % 2)
                sp.dma_start(x_sb[:, TH * u:TH * u + TH, :], x_v[b, :, a:a + TH, :]).then_inc(x_in[u], 16)
            for u in range(U):
                sp.wait_ge(final_done, u + 1)
                b, a = u // 2, TH * (u % 2)
                sp.dma_start(out_v[b, :, a:a + TH, :], g_sb[:, TH * u:TH * u + TH, :]).then_inc(out_stored, 16)
            sp.wait_ge(out_stored, 16 * U)

        @block.gpsimd
        def _(pool):
            chain = [0]

            def link(ins):
                chain[0] += 1
                ins.then_inc(pool_chain, 1)
                pool.wait_ge(pool_chain, chain[0])

            link(nc.gpsimd.memset(ident[:], 0.0))
            nc.gpsimd.affine_select(out=ident[:], in_=ident[:], compare_op=ALU.not_equal, fill=1.0, base=0,
                                    pattern=[[-1, P]], channel_multiplier=1).then_inc(ident_set, 1)
            nc.gpsimd.memset(minus_half[:], -0.5)
            link(nc.gpsimd.memset(minus_one[:], -1.0))

            def rstd(bn, var, r, a, n, eps):
                _, m2 = stats(bn, a, n)
                link(nc.gpsimd.tensor_scalar(var[:, a:a + n], m2, 1.0 / D, eps, ALU.mult, ALU.add))
                return nc.gpsimd.tensor_tensor(r[:, a:a + n], var[:, a:a + n], minus_half[:, 0:n], ALU.pow)

            def ln1(b):
                pool.wait_ge(bn1_done, b + 1)
                rstd(bn1, var1, r1, T * b, T, LN_EPS).then_inc(r1_done, 1)

            def split_biases():
                pool.wait_ge(bias_in, 16 * 4)
                link(nc.gpsimd.tensor_scalar(bias_f[:, 0:2 * P], bias_f[:, 0:2 * P], 1.0, 1.0, ALU.mult, ALU.add))
                link(nc.gpsimd.tensor_copy(bias_hi[:], bias_f[:]))
                link(nc.gpsimd.tensor_tensor(bias_r1[:], bias_f[:], bias_hi[:], ALU.subtract))
                link(nc.gpsimd.tensor_copy(bias_mid[:], bias_r1[:]))
                link(nc.gpsimd.tensor_tensor(bias_r2[:], bias_r1[:], bias_mid[:], ALU.subtract))
                link(nc.gpsimd.tensor_copy(bias_lo[:], bias_r2[:]))
                pool.wait_ge(ident_set, 1)
                for n, part in enumerate((bias_hi, bias_mid, bias_lo)):
                    link(nc.gpsimd.tensor_scalar(bias_m[:, n, :], part[:], ident[0:3, n:n + 1], 0.0, ALU.mult, ALU.add))
                link(nc.gpsimd.tensor_tensor(bias_m[:, 0, :], bias_m[:, 0, :], bias_m[:, 1, :], ALU.add))
                nc.gpsimd.tensor_tensor(bias3[:], bias_m[:, 0, :], bias_m[:, 2, :], ALU.add).then_inc(bias_set, 1)

            def masks():
                link(nc.gpsimd.memset(lower[:], 1.0))
                nc.gpsimd.affine_select(out=lower[:], in_=lower[:], compare_op=ALU.is_gt, fill=0.0, base=0,
                                        pattern=[[1, P]], channel_multiplier=-1).then_inc(lower_set, 1)
                link(nc.gpsimd.memset(head_mask[:], 1.0))
                link(nc.gpsimd.affine_select(out=head_mask[:], in_=head_mask[:], compare_op=ALU.is_ge, fill=0.0, base=0,
                                             pattern=[[-DEPTH, HEADS], [0, DEPTH]], channel_multiplier=1))
                nc.gpsimd.affine_select(out=head_mask[:], in_=head_mask[:], compare_op=ALU.is_ge, fill=0.0,
                                        base=DEPTH - 1, pattern=[[DEPTH, HEADS], [0, DEPTH]],
                                        channel_multiplier=-1).then_inc(mask_set, 1)

            def key_norms(u):
                s = u % 2
                pool.wait_ge(k2_done, u + 1)
                if u >= 2:
                    pool.wait_ge(v_done, u - 1)
                k2 = k2_sb[:, s]
                link(nc.gpsimd.tensor_tensor(k_add4[:, s], k2[:, :, 0:4], k2[:, :, 4:8], ALU.add))
                link(nc.gpsimd.tensor_tensor(k_add2[:, s], k_add4[:, s, :, 0:2], k_add4[:, s, :, 2:4], ALU.add))
                link(nc.gpsimd.tensor_tensor(k_ssq[:, s], k_add2[:, s, :, 0], k_add2[:, s, :, 1], ALU.add))
                link(nc.gpsimd.tensor_scalar(k_ssq[:, s], k_ssq[:, s], 1.0, ATTN_EPS, ALU.mult, ALU.add))
                nc.gpsimd.tensor_tensor(k_rnorm[:, s], k_ssq[:, s], minus_half[:], ALU.pow).then_inc(rnorm_done, 1)

            def add_beta(u):
                pool.wait_ge(x_in[u], 16)
                if u == 0:
                    pool.wait_ge(gb_in, 32)
                a = TH * u
                nc.gpsimd.tensor_tensor(xb_sb[:, a:a + TH], x_sb[:, a:a + TH],
                                        beta_sb[:].unsqueeze(1).to_broadcast([P, TH, D]), ALU.add).then_inc(xb_done, 1)

            def y_scale(u):
                a = TH * u
                pool.wait_ge(bny_done, u + 1)
                link(rstd(bny, vary, ry, a, TH, ATTN_EPS))
                mean, _ = stats(bny, a, TH)
                link(nc.gpsimd.tensor_tensor(neg_ry[:, a:a + TH], ry[:, a:a + TH], minus_one[:, 0:TH], ALU.mult))
                nc.gpsimd.tensor_tensor(shift_y[:, a:a + TH], neg_ry[:, a:a + TH], mean, ALU.mult).then_inc(ry_done, 1)

            def residual(u):
                a = TH * u
                pool.wait_ge(yn_done, u + 1)
                link(nc.gpsimd.tensor_tensor(yn_sb[:, u % 2], yn_sb[:, u % 2],
                                             gamma_sb[:].unsqueeze(1).to_broadcast([P, TH, D]), ALU.mult))
                pool.wait_ge(xb_done, u + 1)
                nc.gpsimd.tensor_tensor(xb_sb[:, a:a + TH], xb_sb[:, a:a + TH], yn_sb[:, u % 2],
                                        ALU.add).then_inc(x1_done, 1)

            def ln3(u):
                pool.wait_ge(bn3_done, u + 1)
                rstd(bn3, var3, r3, TH * u, TH, LN_EPS).then_inc(r3_done, 1)

            def final(u):
                a = TH * u
                pool.wait_ge(merged, u // 2 + 1)
                nc.gpsimd.tensor_tensor(g_sb[:, a:a + TH], g_sb[:, a:a + TH], xb_sb[:, a:a + TH],
                                        ALU.add).then_inc(final_done, 1)

            ln1(0)
            split_biases()
            ln1(1)
            masks()
            for b in range(B):
                add_beta(2 * b)
                if b + 2 < B:
                    ln1(b + 2)
                add_beta(2 * b + 1)
                key_norms(2 * b)
                key_norms(2 * b + 1)
            for s in range(U + RANK_LAG + 1):
                if s < U:
                    y_scale(s)
                if 1 <= s <= U:
                    ln3(s - 1)
                if s < U:
                    residual(s)
                if s >= 7 and s % 2:
                    final(s - 7)
                    final(s - 6)

        @block.scalar
        def _(act):
            act.dma_start(wq_sb[:], wq).then_inc(wq_in, 16)
            act.dma_start(wkv_sb[:, 0:P], wk).then_inc(wkv_in, 16)
            act.dma_start(wkv_sb[:, P:2 * P], wv).then_inc(wkv_in, 16)
            for n, vec in enumerate((bq, bk, bv, bo)):
                act.dma_start(bias_f[:, n * P:(n + 1) * P], vec.partition_broadcast(3)).then_inc(bias_in, 16)
            act.dma_start(beta_sb[:], beta.partition_broadcast(P)).then_inc(gb_in, 16)
            act.dma_start(gamma_sb[:], gamma.partition_broadcast(P)).then_inc(gb_in, 16)
            act.dma_start(wo_sb[:], wo).then_inc(wo_in, 16)
            act.dma_start(wz_sb[:, 0:P], w_block).then_inc(wz_in, 16)
            act.dma_start(wz_sb[:, P:P + 1], w_router.unsqueeze(1)).then_inc(wz_in, 16)

            def copy_hT(u):
                act.wait_ge(t_full, t_at["h", u] + 1)
                nc.scalar.copy(hT[:, u], t_bank(("h", u))).then_inc(t_free, 1)

            def exp_q_half(u):
                act.wait_ge(q_full, u + 1)
                if u == 0:
                    act.wait_ge(dve_const, 1)
                if u >= 2:
                    act.wait_ge(q_done, u - 1)
                nc.scalar.activation(exp_q[:, u % 2], bank[:, Q_BANKS[u % 2], :], ACT.Exp,
                                     bias=minus1[:, 0:1]).then_inc(expq_done, 1)

            def exp_k_half(u):
                act.wait_ge(kv_full, u + 1)
                if u >= 2:
                    act.wait_ge(k_done, u - 1)
                nc.scalar.activation(exp_k[:, u % 2].rearrange("p (t d) -> p t d", d=D), kv_ps(u)[:, :, 0:P], ACT.Exp,
                                     bias=minus1[:, 0:1]).then_inc(expk_done, 1)

            def square_k(u):
                act.wait_ge(k_done, u + 1)
                if u >= 2:
                    act.wait_ge(rnorm_done, u - 1)
                nc.scalar.activation(k2_sb[:, u % 2].rearrange("p h e -> p (h e)"),
                                     k_sb[:, u % 4].rearrange("p t d -> p (t d)"), ACT.Square).then_inc(k2_done, 1)

            def copy_M(b):
                act.wait_ge(t_full, t_at["M", b] + 1)
                nc.scalar.copy(M_sb[:, b], t_bank(("M", b))[:, P:2 * P]).then_inc(t_free, 1)

            def y_norm(u):
                act.wait_ge(ry_done, u + 1)
                if u >= 2:
                    act.wait_ge(x1_done, u - 1)
                for t in range(TH):
                    n = TH * u + t
                    last = nc.scalar.activation(yn_sb[:, u % 2, t], bank[:, Y_BANKS[u % 4], t * P:(t + 1) * P],
                                                ACT.Identity, bias=shift_y[:, n:n + 1], scale=ry[:, n:n + 1])
                last.then_inc(yn_done, 1)

            def copy_h2T(u):
                act.wait_ge(t_full, t_at["h2", u] + 1)
                if u >= 2:
                    act.wait_ge(z_full, u - 1)
                nc.scalar.copy(h2T[:, u % 2], t_bank(("h2", u))).then_inc(t_free, 1)

            def gelu(u):
                act.wait_ge(z_full, u + 1)
                act.wait_ge(s_col_done, u + 1)
                nc.scalar.activation(g_sb[:, TH * u:TH * u + TH].rearrange("p (a t) d -> p a t d", a=2),
                                     z_ps()[:, :, :, 0:P], ACT.Gelu_apprx_tanh).then_inc(gelu_done, 1)

            def copy_s_row(u):
                b = u // 2
                act.wait_ge(t_full, t_at["s", u] + 1)
                if b >= 2:
                    act.wait_ge(beats_done, b - 1)
                a = HW * (u % 2)
                nc.scalar.copy(s_row[:, b % 2, a:a + HW], t_bank(("s", u))).then_inc(t_free, 1)

            def copy_rank(b):
                act.wait_ge(t_full, t_at["r", b] + 1)
                if b >= 2:
                    act.wait_ge(dropped_done, b - 1)
                nc.scalar.copy(rank_sb[:, b % 2], t_bank(("r", b))[:, 0:T]).then_inc(t_free, 1)

            for b in range(B):
                copy_hT(2 * b)
                copy_hT(2 * b + 1)
                exp_q_half(2 * b)
                exp_q_half(2 * b + 1)
                if b:
                    copy_M(b - 1)
                exp_k_half(2 * b)
                exp_k_half(2 * b + 1)
                square_k(2 * b)
                square_k(2 * b + 1)
            copy_M(B - 1)
            for s in range(U + RANK_LAG):
                if s < U:
                    y_norm(s)
                if 2 <= s < U + 2:
                    copy_h2T(s - 2)
                    gelu(s - 2)
                if 3 <= s < U + 3:
                    copy_s_row(s - 3)
                if s >= RANK_LAG and (s - RANK_LAG) % 2 == 0:
                    copy_rank((s - RANK_LAG) // 2)

        @block.vector
        def _(dve):
            nc.vector.memset(ones_col[:], 1.0)
            nc.vector.memset(ones3[:], 1.0)
            nc.vector.memset(minus1[:], -1.0).then_inc(dve_const, 1)

            def ln1(b):
                for g in range(T // 2 * b, T // 2 * (b + 1)):
                    if g % 2 == 0:
                        dve.wait_ge(x_in[g // 2], 16)
                    last = nc.vector.bn_stats(bn1[:, g, :], pairs(x_sb, g))
                last.then_inc(bn1_done, 1)

            def normalise1(b):
                mean, _ = stats(bn1, 0, B * T)
                dve.wait_ge(r1_done, b + 1)
                for n in range(T * b, T * (b + 1)):
                    last = nc.vector.tensor_scalar(norm_sb[:, n], x_sb[:, n], mean[:, n:n + 1], r1[:, n:n + 1],
                                                   ALU.subtract, ALU.mult)
                    if n % TH == TH - 1:
                        last.then_inc(h_done, 1)

            def q_half(u):
                dve.wait_ge(expq_done, u + 1)
                nc.vector.scalar_tensor_tensor(out=qT[:, u], in0=exp_q[:, u % 2], scalar=1.0,
                                               in1=bank[:, Q_BANKS[u % 2], :], op0=ALU.min, op1=ALU.max).then_inc(q_done, 1)

            def k_half(u):
                dve.wait_ge(expk_done, u + 1)
                if u >= 4:
                    dve.wait_ge(vk_full, u // 2 - 1)
                nc.vector.scalar_tensor_tensor(out=k_sb[:, u % 4],
                                               in0=exp_k[:, u % 2].rearrange("p (t d) -> p t d", d=D), scalar=1.0,
                                               in1=kv_ps(u)[:, :, 0:P], op0=ALU.min, op1=ALU.max).then_inc(k_done, 1)

            def v_half(u):
                dve.wait_ge(rnorm_done, u + 1)
                if u >= 4:
                    dve.wait_ge(vk_full, u // 2 - 1)
                rn = k_rnorm[:, u % 2].rearrange("p (t h) -> p t h", t=TH).unsqueeze(3).to_broadcast([P, TH, HEADS, DEPTH])
                nc.vector.tensor_tensor(v_sb[:, u % 4].rearrange("p t (h e) -> p t h e", e=DEPTH),
                                        kv_ps(u)[:, :, P:2 * P].rearrange("p t (h e) -> p t h e", e=DEPTH), rn,
                                        ALU.mult).then_inc(v_done, 1)

            def mask_vk(b):
                if b == 0:
                    dve.wait_ge(mask_set, 1)
                dve.wait_ge(vk_full, b + 1)
                nc.vector.tensor_tensor(vk_sb[:, b % 2], t_bank(("M", b))[:, 0:P], head_mask[:], ALU.mult).then_inc(vk_done, 1)

            def y_stats(u):
                dve.wait_ge(y_full, u + 1)
                y = bank[:, Y_BANKS[u % 4], :].rearrange("p (t d) -> p t d", d=D)
                for g in range(TH // 2):
                    last = nc.vector.bn_stats(bny[:, TH // 2 * u + g, :], pairs(y, g))
                last.then_inc(bny_done, 1)

            def x1_stats(u):
                dve.wait_ge(x1_done, u + 1)
                for g in range(TH // 2 * u, TH // 2 * (u + 1)):
                    last = nc.vector.bn_stats(bn3[:, g, :], pairs(xb_sb, g))
                last.then_inc(bn3_done, 1)

            def normalise3(u):
                mean, _ = stats(bn3, 0, B * T)
                dve.wait_ge(r3_done, u + 1)
                for n in range(TH * u, TH * u + TH):
                    last = nc.vector.tensor_scalar(norm_sb[:, n], xb_sb[:, n], mean[:, n:n + 1], r3[:, n:n + 1],
                                                   ALU.subtract, ALU.mult)
                last.then_inc(h2_done, 1)

            def score_cols(u):
                dve.wait_ge(z_full, u + 1)
                nc.vector.tensor_copy(s_col[:, TH * u:TH * u + TH].rearrange("p (a t) -> p a t", a=2),
                                      z_ps()[:, :, :, P]).then_inc(s_col_done, 1)

            def compare(b, J0, J1):
                s = b % 2
                if J0 == 0:
                    dve.wait_ge(t_free, t_at["s", 2 * b + 1] + 1)
                    if b == 0:
                        dve.wait_ge(lower_set, 1)
                    if b >= 2:
                        dve.wait_ge(t_full, t_at["r", b - 2] + 1)
                for J in range(J0, J1):
                    s_j = s_col[:, T * b + J:T * b + J + 1]
                    a = P * (J + 1)
                    nc.vector.tensor_scalar(beats[:, s, J, 0:a], s_row[:, s, 0:a], s_j, None, ALU.is_lt)
                    if J < T - 1:
                        nc.vector.tensor_scalar(beats[:, s, J, a:], s_row[:, s, a:], s_j, None, ALU.is_le)
                    last = nc.vector.scalar_tensor_tensor(out=ties[:, s, J], in0=s_row[:, s, P * J:a], scalar=s_j,
                                                          in1=lower[:], op0=ALU.is_equal, op1=ALU.mult)
                if J1 == T:
                    last.then_inc(beats_done, 1)

            def merge(b):
                dve.wait_ge(t_free, t_at["r", b] + 1)
                nc.vector.tensor_scalar(dropped[:, b % 2], rank_sb[:, b % 2], KEEP - 0.5, None, ALU.is_gt).then_inc(dropped_done, 1)
                dve.wait_ge(dropped_done, b + 1)
                dve.wait_ge(gelu_done, 2 * b + 2)
                nc.vector.copy_predicated(g_sb[:, T * b:T * (b + 1)],
                                          dropped[:, b % 2].unsqueeze(2).to_broadcast([P, T, D]),
                                          norm_sb[:, T * b:T * (b + 1)]).then_inc(merged, 1)

            ln1(0)
            normalise1(0)
            ln1(1)
            normalise1(1)
            for b in range(B):
                q_half(2 * b)
                q_half(2 * b + 1)
                if b:
                    mask_vk(b - 1)
                k_half(2 * b)
                k_half(2 * b + 1)
                if b + 2 < B:
                    ln1(b + 2)
                    normalise1(b + 2)
                v_half(2 * b)
                v_half(2 * b + 1)
            mask_vk(B - 1)
            for s in range(U + RANK_LAG + 1):
                if s < U:
                    y_stats(s)
                if 1 <= s <= U:
                    x1_stats(s - 1)
                    normalise3(s - 1)
                if 2 <= s < U + 2:
                    score_cols(s - 2)
                if s >= 4 and s % 2 == 0 and (s - 4) // 2 < B:
                    compare((s - 4) // 2, 0, T // 2)
                if s >= 5 and s % 2 and (s - 5) // 2 < B:
                    compare((s - 5) // 2, T // 2, T)
                if s >= 7 and s % 2:
                    merge((s - 7) // 2)

        @block.tensor
        def _(pe):
            def take_t(use):
                if t_at[use] >= 2:
                    pe.wait_ge(t_free, t_at[use] - 1)

            def transpose_h(u):
                pe.wait_ge(h_done, u + 1)
                if u == 0:
                    pe.wait_ge(ident_set, 1)
                take_t(("h", u))
                for t in range(TH):
                    last = nc.tensor.transpose(t_bank(("h", u))[:, t * P:(t + 1) * P], norm_sb[:, TH * u + t], ident[:])
                last.then_inc(t_full, 1)

            def q_proj(u):
                pe.wait_ge(t_free, t_at["h", u] + 1)
                if u == 0:
                    pe.wait_ge(wq_in, 16)
                    pe.wait_ge(bias_set, 1)
                    pe.wait_ge(dve_const, 1)
                if u >= 2:
                    pe.wait_ge(q_done, u - 1)
                o = bank[:, Q_BANKS[u % 2], :]
                nc.tensor.matmul(o, wq_sb[:], hT[:, u], start=True, stop=False)
                nc.tensor.matmul(o, bias3[:, 0:P], ones3[:], start=False, stop=True).then_inc(q_full, 1)

            def kv_proj(u):
                if u == 0:
                    pe.wait_ge(wkv_in, 32)
                if u >= 2:
                    pe.wait_ge(v_done, u - 1)
                for t in range(TH):
                    o = kv_ps(u)[:, t, :]
                    nc.tensor.matmul(o, hT[:, u, t * P:(t + 1) * P], wkv_sb[:], start=True, stop=False)
                    last = nc.tensor.matmul(o, ones3[:, 0:P], bias3[:, P:3 * P], start=False, stop=True)
                last.then_inc(kv_full, 1)

            def attention_matrix(b):
                pe.wait_ge(v_done, 2 * b + 2)
                take_t(("M", b))
                o = t_bank(("M", b))
                for t in range(T):
                    s = (T * b + t) // TH % 4
                    last = nc.tensor.matmul(o[:, 0:P], v_sb[:, s, t % TH], k_sb[:, s, t % TH], start=(t == 0), stop=(t == T - 1))
                last.then_inc(vk_full, 1)

            def attention_out(b):
                if b == 0:
                    pe.wait_ge(wo_in, 16)
                pe.wait_ge(vk_done, b + 1)
                nc.tensor.matmul(t_bank(("M", b))[:, P:2 * P], vk_sb[:, b % 2], wo_sb[:], start=True, stop=True).then_inc(t_full, 1)

            def y_half(u):
                b = u // 2
                pe.wait_ge(t_free, t_at["M", b] + 1)
                pe.wait_ge(q_done, u + 1)
                if u >= 4:
                    pe.wait_ge(yn_done, u - 3)
                elif u >= 2:
                    pe.wait_ge(v_done, U)
                for t in range(TH):
                    o = bank[:, Y_BANKS[u % 4], t * P:(t + 1) * P]
                    nc.tensor.matmul(o, qT[:, u, t * P:(t + 1) * P], M_sb[:, b], start=True, stop=False)
                    nc.tensor.matmul(o, hT[:, u, t * P:(t + 1) * P], ident[:], start=False, stop=False)
                    last = nc.tensor.matmul(o, ones3[:, 0:P], bias3[:, 3 * P:4 * P], start=False, stop=True)
                last.then_inc(y_full, 1)

            def transpose_h2(u):
                pe.wait_ge(h2_done, u + 1)
                take_t(("h2", u))
                for t in range(TH):
                    last = nc.tensor.transpose(t_bank(("h2", u))[:, t * P:(t + 1) * P], norm_sb[:, TH * u + t], ident[:])
                last.then_inc(t_full, 1)

            def z_half(u):
                pe.wait_ge(t_free, t_at["h2", u] + 1)
                if u == 0:
                    pe.wait_ge(wz_in, 32)
                    pe.wait_ge(v_done, U)
                if u >= 1:
                    pe.wait_ge(gelu_done, u)
                    pe.wait_ge(s_col_done, u)
                for t in range(TH):
                    last = nc.tensor.matmul(z_ps()[:, t // 2, t % 2, :], h2T[:, u % 2, t * P:(t + 1) * P], wz_sb[:],
                                            start=True, stop=True)
                last.then_inc(z_full, 1)

            def score_rows(u):
                pe.wait_ge(s_col_done, u + 1)
                take_t(("s", u))
                for t in range(TH):
                    n = TH * u + t
                    last = nc.tensor.transpose(t_bank(("s", u))[:, t * P:(t + 1) * P],
                                               s_col[:, n:n + 1].to_broadcast([P, P]), ident[:])
                last.then_inc(t_full, 1)

            def rank(b):
                s = b % 2
                pe.wait_ge(beats_done, b + 1)
                take_t(("r", b))
                o = t_bank(("r", b))
                for i in range(T):
                    for J in range(T):
                        nc.tensor.matmul(o[:, i:i + 1], beats[:, s, J, i * P:(i + 1) * P], ones_col[:],
                                         start=(J == 0), stop=False)
                    last = nc.tensor.matmul(o[:, i:i + 1], ties[:, s, i], ones_col[:], start=False, stop=True)
                last.then_inc(t_full, 1)

            for b in range(B):
                transpose_h(2 * b)
                transpose_h(2 * b + 1)
                q_proj(2 * b)
                q_proj(2 * b + 1)
                if b:
                    attention_matrix(b - 1)
                    attention_out(b - 1)
                kv_proj(2 * b)
                kv_proj(2 * b + 1)
            attention_matrix(B - 1)
            attention_out(B - 1)
            for s in range(U + RANK_LAG):
                if s < U:
                    y_half(s)
                if 2 <= s < U + 2:
                    transpose_h2(s - 2)
                    z_half(s - 2)
                if 3 <= s < U + 3:
                    score_rows(s - 3)
                if s >= RANK_LAG and (s - RANK_LAG) % 2 == 0:
                    rank((s - RANK_LAG) // 2)


_INS = ['L0_attn_x', 'L0_attn_Wq', 'L0_attn_bq', 'L0_attn_Wk', 'L0_attn_bk', 'L0_attn_Wv', 'L0_attn_bv', 'L0_attn_Wo',
        'L0_attn_bo', 'L0_attn_gamma', 'L0_attn_beta', 'L0_ffn_w_router', 'L0_ffn_w_block']
_OUTS = [((4, 1024, 128), 'float32')]


def kernel(**inputs):
    import numpy as _np
    import concourse.bacc as _bacc
    from concourse import mybir as _mybir
    from concourse.bass_utils import run_bass_kernel_spmd as _run

    nc = _bacc.Bacc("TRN2", target_bir_lowering=False, num_devices=1)
    arrays, args = {}, []
    for name in _INS:
        a = _np.ascontiguousarray(inputs[name])
        arrays[f"in_{name}_dram"] = a
        args.append(nc.dram_tensor(f"in_{name}_dram", a.shape, _mybir.dt.from_np(a.dtype), kind="ExternalInput").ap())
    for i, (shape, dtype) in enumerate(_OUTS):
        dt = _mybir.dt.from_np(_np.dtype(dtype))
        args.append(nc.dram_tensor(f"out_{i}_dram", shape, dt, kind="ExternalOutput").ap())
    preln_linear_attention_mod_ffn(nc, *args)
    r = _run(nc, [arrays], core_ids=[0])
    got = tuple(r.results[0][f"out_{i}_dram"] for i in range(len(_OUTS)))
    return got[0]
```

```python
from contextlib import ExitStack

import concourse.bass as bass
from concourse import mybir

ALU = mybir.AluOpType
ACT = mybir.ActivationFunctionType
F32 = mybir.dt.float32
BF16 = mybir.dt.bfloat16
I32 = mybir.dt.int32

P = 128
HEADS, DEPTH = 16, 8
LN_EPS = 1e-5
ATTN_EPS = 1e-6
CAPACITY = 0.75
TH = 4


def preln_linear_attention_mod_ffn(nc, x, wq, bq, wk, bk, wv, bv, wo, bo, gamma, beta, w_router, w_block, out):
    B, L, D = x.shape
    assert D == P and HEADS * DEPTH == D and L % (2 * TH * P) == 0
    T = L // P
    U = B * T // TH
    HW = TH * P
    KEEP = max(1, int(L * CAPACITY))
    assert T == 2 * TH
    VKL = 7
    OFF = 10
    XL = 2
    CL = XL + 3
    RL = CL + 2
    ROUNDS = OFF + U + RL

    x_v = x.rearrange("b (t p) d -> b p t d", p=P)
    out_v = out.rearrange("b (t p) d -> b p t d", p=P)

    with ExitStack() as ctx:
        def sb(name, shape, dt=F32):
            return ctx.enter_context(nc.sbuf_tensor(name, shape, dt))

        def sem(name):
            return ctx.enter_context(nc.semaphore(name))

        x_sb = sb("x_sb", [P, B * T, D])
        norm_sb = sb("norm_sb", [P, B * T, D])
        hT = sb("hT", [P, U, HW])
        qT = sb("qT", [P, U, HW])
        exp_q = sb("exp_q", [P, 2, HW])
        exp_k = sb("exp_k", [P, 2, HW])
        k_sb = sb("k_sb", [P, U, TH, D])
        k2_sb = sb("k2_sb", [P, 2, TH * HEADS, DEPTH])
        k_add4 = sb("k_add4", [P, 2, TH * HEADS, 4])
        k_add2 = sb("k_add2", [P, 2, TH * HEADS, 2])
        k_ssq = sb("k_ssq", [P, 2, T * HEADS])
        k_seed = sb("k_seed", [P, 2, T * HEADS])
        k_tmp = sb("k_tmp", [P, T * HEADS])
        k_rnorm = sb("k_rnorm", [P, T * HEADS])
        v_sb = sb("v_sb", [P, U, TH, D])
        vk_sb = sb("vk_sb", [P, 2, P])
        M_sb = sb("M_sb", [P, B, P])
        yn_sb = sb("yn_sb", [P, 2, TH, D])
        h2T = sb("h2T", [P, 2, HW])
        g_sb = sb("g_sb", [P, B * T, D])
        s_col = sb("s_col", [P, B * T])
        s_row = sb("s_row", [P, 2, T * P])
        beats = sb("beats", [P, 2, T, T * P], BF16)
        ties = sb("ties", [P, 2, T, P], BF16)
        rank_sb = sb("rank_sb", [P, 2, T])
        dropped = sb("dropped", [P, 2, T], I32)
        bn1 = sb("bn1", [P, B, T // 2, 6])
        bn2 = sb("bn2", [P, U + XL, T // 2, 6])
        r1 = sb("r1", [P, B, T])
        var1, root1, root1b = sb("var1", [P, B, T]), sb("root1", [P, B, T]), sb("root1b", [P, B, T])
        bits1 = sb("bits1", [P, B, T], I32)
        shift1 = sb("shift1", [P, B, T])
        r2 = sb("r2", [P, U + XL, T])
        shift2 = sb("shift2", [P, U + XL, T])
        var = sb("var", [P, T])
        root = sb("root", [P, T])
        root2 = sb("root2", [P, T])
        bits = sb("bits", [P, T], I32)
        eps1 = sb("eps1", [P, B, T])
        eps2 = sb("eps2", [P, T])
        ident = sb("ident", [P, P])
        lower = sb("lower", [P, P])
        head_mask = sb("head_mask", [P, P])
        minus1 = sb("minus1", [P, 1])
        ones_col = sb("ones_col", [P, 1], BF16)
        ones3 = sb("ones3", [3, HW], BF16)
        wq_sb = sb("wq_sb", [P, P])
        wkv_sb = sb("wkv_sb", [P, 2 * P])
        wo_sb = sb("wo_sb", [P, P])
        wz_sb = sb("wz_sb", [P, P + 1])
        gamma_sb = sb("gamma_sb", [P, P])
        beta_sb = sb("beta_sb", [P, P])
        bias_f = sb("bias_f", [3, 4 * P])
        bias_cut = sb("bias_cut", [3, 4 * P], BF16)
        minus_later = sb("minus_later", [3, 2])
        bias3 = sb("bias3", [3, 4 * P], BF16)

        bank = ctx.enter_context(nc.psum_tensor("bank", [P, 8, HW], F32))
        T_BANKS = (0, 1)
        Q_BANKS = (2, 3)
        Y_BANKS = (2, 3, 6, 7)

        def kv_ps(u):
            a = 4 + 2 * (u % 2)
            return bank[:, a:a + 2, :].rearrange("p a (t c) -> p (a t) c", c=2 * P)

        def z_ps():
            return bank[:, 4:6, 0:2 * (P + 1)].rearrange("p a (t c) -> p a t c", c=P + 1)

        x_in = [sem(f"x_in{b}") for b in range(2 * B)]
        wq_in, wkv_in, wo_in, wz_in = sem("wq_in"), sem("wkv_in"), sem("wo_in"), sem("wz_in")
        bias_in, gb_in = sem("bias_in"), sem("gb_in")
        out_stored = sem("out_stored")
        pool_chain = sem("pool_chain")
        dve_chain = sem("dve_chain")
        ident_set, lower_set, mask_set = sem("ident_set"), sem("lower_set"), sem("mask_set")
        dve_const, bias_set = sem("dve_const"), sem("bias_set")
        r1_done, h_done, h_done_act = sem("r1_done"), sem("h_done"), sem("h_done_act")
        t_full, t_free = sem("t_full"), sem("t_free")
        vk_full, vk_done = sem("vk_full"), sem("vk_done")
        hT_done, q_full, expq_done, q_done = sem("hT_done"), sem("q_full"), sem("expq_done"), sem("q_done")
        kv_full, expk_done, k_done, k2_done = sem("kv_full"), sem("expk_done"), sem("k_done"), sem("k2_done")
        rnorm_done, kn_done, v_done = sem("rnorm_done"), sem("kn_done"), sem("v_done")
        xb_done = sem("xb_done")
        ssq_done, seed_done, ln_done = sem("ssq_done"), sem("seed_done"), sem("ln_done")
        rstd_step, later_set = sem("rstd_step"), sem("later_set")
        y_full, r2_done, yn_done = sem("y_full"), sem("r2_done"), sem("yn_done")
        x1_done, h2_done = sem("x1_done"), sem("h2_done")
        h2T_done, z_full, gelu_done, s_col_done = sem("h2T_done"), sem("z_full"), sem("gelu_done"), sem("s_col_done")
        beats_done = sem("beats_done")
        dropped_done, merged, final_done = sem("dropped_done"), sem("merged"), sem("final_done")

        t_uses = []
        for i in range(ROUNDS):
            s = i - OFF
            if i < U:
                t_uses += [("h", i)]
            if i >= VKL and (i - VKL) % 2 == 0 and (i - VKL) // 2 < B:
                t_uses += [("M", (i - VKL) // 2)]
            if XL + 2 <= s < U + XL + 2:
                t_uses += [("s", s - XL - 2)]
            if XL + 1 <= s < U + XL + 1:
                t_uses += [("h2", s - XL - 1)]
            if s >= RL and (s - RL) % 2 == 0 and (s - RL) // 2 < B:
                t_uses += [("r", (s - RL) // 2)]
        t_at = {use: n for n, use in enumerate(t_uses)}

        def t_bank(use):
            return bank[:, T_BANKS[t_at[use] % 2], :]

        def stats(bn, group):
            v = bn[:, group].rearrange("p g (e s) -> p (g e) s", s=3)
            return v[:, :, 1], v[:, :, 2]

        def pairs(ap, g):
            return ap[:, 2 * g:2 * g + 2, :].rearrange("p t d -> p d t")

        block = ctx.enter_context(nc.Block())

        @block.sync
        def _(sp):
            for u in range(U):
                b, a = u // 2, TH * (u % 2)
                sp.dma_start(x_sb[:, TH * u:TH * u + TH, :], x_v[b, :, a:a + TH, :]).then_inc(x_in[u], 16)
                if u == 0:
                    sp.dma_start(wq_sb[:], wq).then_inc(wq_in, 16)
                if u == 1:
                    sp.dma_start(wkv_sb[:, 0:P], wk).then_inc(wkv_in, 16)
                    sp.dma_start(wkv_sb[:, P:2 * P], wv).then_inc(wkv_in, 16)
            for u in range(U):
                sp.wait_ge(final_done, u + 1)
                b, a = u // 2, TH * (u % 2)
                sp.dma_start(out_v[b, :, a:a + TH, :], g_sb[:, TH * u:TH * u + TH, :]).then_inc(out_stored, 16)
            sp.wait_ge(out_stored, 16 * U)

        @block.gpsimd
        def _(pool):
            chain = [0]

            def link(ins):
                chain[0] += 1
                ins.then_inc(pool_chain, 1)
                pool.wait_ge(pool_chain, chain[0])

            link(nc.gpsimd.memset(ident[:], 0.0))
            nc.gpsimd.affine_select(out=ident[:], in_=ident[:], compare_op=ALU.not_equal, fill=1.0, base=0,
                                    pattern=[[-1, P]], channel_multiplier=1).then_inc(ident_set, 1)
            def masks():
                link(nc.gpsimd.memset(minus_later[:], -1.0))
                nc.gpsimd.affine_select(out=minus_later[:], in_=minus_later[:], compare_op=ALU.is_ge, fill=0.0, base=-1,
                                        pattern=[[-1, 2]], channel_multiplier=1).then_inc(later_set, 1)
                link(nc.gpsimd.memset(lower[:], 1.0))
                nc.gpsimd.affine_select(out=lower[:], in_=lower[:], compare_op=ALU.is_gt, fill=0.0, base=0,
                                        pattern=[[1, P]], channel_multiplier=-1).then_inc(lower_set, 1)
                link(nc.gpsimd.memset(head_mask[:], 1.0))
                link(nc.gpsimd.affine_select(out=head_mask[:], in_=head_mask[:], compare_op=ALU.is_ge, fill=0.0, base=0,
                                             pattern=[[-DEPTH, HEADS], [0, DEPTH]], channel_multiplier=1))
                nc.gpsimd.affine_select(out=head_mask[:], in_=head_mask[:], compare_op=ALU.is_ge, fill=0.0,
                                        base=DEPTH - 1, pattern=[[DEPTH, HEADS], [0, DEPTH]],
                                        channel_multiplier=-1).then_inc(mask_set, 1)

            def key_sums(u):
                s, b = u % 2, u // 2
                pool.wait_ge(k2_done, u + 1)
                k2 = k2_sb[:, s]
                o = k_ssq[:, b % 2, s * TH * HEADS:(s + 1) * TH * HEADS]
                link(nc.gpsimd.tensor_tensor(k_add4[:, s], k2[:, :, 0:4], k2[:, :, 4:8], ALU.add))
                link(nc.gpsimd.tensor_tensor(k_add2[:, s], k_add4[:, s, :, 0:2], k_add4[:, s, :, 2:4], ALU.add))
                if u % 2 == 0 and b >= 2:
                    pool.wait_ge(rnorm_done, b - 1)
                link(nc.gpsimd.tensor_tensor(o, k_add2[:, s, :, 0], k_add2[:, s, :, 1], ALU.add))
                nc.gpsimd.tensor_scalar(o, o, 1.0, ATTN_EPS, ALU.mult, ALU.add).then_inc(ssq_done, 1)

            def add_beta(u):
                pool.wait_ge(h_done_act if u % 2 else h_done, u // 2 + 1)
                if u == 0:
                    pool.wait_ge(gb_in, 32)
                a = TH * u
                nc.gpsimd.tensor_tensor(x_sb[:, a:a + TH], x_sb[:, a:a + TH],
                                        beta_sb[:].unsqueeze(1).to_broadcast([P, TH, D]), ALU.add).then_inc(xb_done, 1)

            def residual(u):
                a = TH * u
                pool.wait_ge(yn_done, u + 1)
                link(nc.gpsimd.tensor_tensor(yn_sb[:, u % 2], yn_sb[:, u % 2],
                                             gamma_sb[:].unsqueeze(1).to_broadcast([P, TH, D]), ALU.mult))
                pool.wait_ge(xb_done, u + 1)
                nc.gpsimd.tensor_tensor(x_sb[:, a:a + TH], x_sb[:, a:a + TH], yn_sb[:, u % 2],
                                        ALU.add).then_inc(x1_done, 1)

            def final(u):
                a = TH * u
                pool.wait_ge(merged, u // 2 + 1)
                nc.gpsimd.tensor_tensor(g_sb[:, a:a + TH], g_sb[:, a:a + TH], x_sb[:, a:a + TH],
                                        ALU.add).then_inc(final_done, 1)

            masks()
            for i in range(ROUNDS):
                s = i - OFF
                if 2 <= i < U + 2:
                    key_sums(i - 2)
                    add_beta(i - 2)
                if 0 <= s < U:
                    residual(s)
                if s >= RL + 1 and (s - RL) % 2:
                    final(s - RL - 1)
                    final(s - RL)

        @block.scalar
        def _(act):
            nc.scalar.preload_act_table_set("natural_log_exp_and_others")
            for n, vec in enumerate((bq, bk, bv, bo)):
                act.dma_start(bias_f[:, n * P:(n + 1) * P], vec.partition_broadcast(3)).then_inc(bias_in, 16)
            act.dma_start(beta_sb[:], beta.partition_broadcast(P)).then_inc(gb_in, 16)
            act.dma_start(gamma_sb[:], gamma.partition_broadcast(P)).then_inc(gb_in, 16)
            act.dma_start(wo_sb[:], wo).then_inc(wo_in, 16)
            act.dma_start(wz_sb[:, 0:P], w_block).then_inc(wz_in, 16)
            act.dma_start(wz_sb[:, P:P + 1], w_router.unsqueeze(1)).then_inc(wz_in, 16)

            def normalise1(b):
                act.wait_ge(r1_done, 1 if b == 0 else 2)
                for t in range(TH, T):
                    last = nc.scalar.activation(norm_sb[:, T * b + t], x_sb[:, T * b + t], ACT.Identity,
                                                bias=shift1[:, b, t:t + 1], scale=r1[:, b, t:t + 1])
                last.then_inc(h_done_act, 1)

            def copy_hT(u):
                act.wait_ge(t_full, t_at["h", u] + 1)
                nc.scalar.copy(hT[:, u], t_bank(("h", u))).then_inc(t_free, 1)

            def exp_q_half(u):
                act.wait_ge(q_full, u + 1)
                if u == 0:
                    act.wait_ge(dve_const, 1)
                if u >= 2:
                    act.wait_ge(q_done, u - 1)
                nc.scalar.activation(exp_q[:, u % 2], bank[:, Q_BANKS[u % 2], :], ACT.Exp,
                                     bias=minus1[:, 0:1]).then_inc(expq_done, 1)

            def exp_k_half(u):
                act.wait_ge(kv_full, u + 1)
                if u >= 2:
                    act.wait_ge(k_done, u - 1)
                nc.scalar.activation(exp_k[:, u % 2].rearrange("p (t d) -> p t d", d=D), kv_ps(u)[:, :, 0:P], ACT.Exp,
                                     bias=minus1[:, 0:1]).then_inc(expk_done, 1)

            def copy_v(u):
                act.wait_ge(k_done, u + 1)
                nc.scalar.copy(v_sb[:, u], kv_ps(u)[:, :, P:2 * P]).then_inc(v_done, 1)

            def square_k(u):
                act.wait_ge(k_done, u + 1)
                if u >= 2:
                    act.wait_ge(ssq_done, u - 1)
                nc.scalar.activation(k2_sb[:, u % 2].rearrange("p h e -> p (h e)"),
                                     k_sb[:, u].rearrange("p t d -> p (t d)"), ACT.Square).then_inc(k2_done, 1)

            def seed_norms(b):
                act.wait_ge(ssq_done, 2 * b + 2)
                if b >= 2:
                    act.wait_ge(rnorm_done, b - 1)
                nc.scalar.activation(k_seed[:, b % 2], k_ssq[:, b % 2], ACT.Ln).then_inc(ln_done, 1)
                act.wait_ge(ln_done, b + 1)
                nc.scalar.activation(k_seed[:, b % 2], k_seed[:, b % 2], ACT.Exp, scale=-0.5).then_inc(seed_done, 1)

            def copy_M(b):
                act.wait_ge(t_full, t_at["M", b] + 1)
                nc.scalar.copy(M_sb[:, b], t_bank(("M", b))[:, P:2 * P]).then_inc(t_free, 1)

            def y_norm(u):
                act.wait_ge(r2_done, u + 1)
                if u >= 2:
                    act.wait_ge(x1_done, u - 1)
                for t in range(TH):
                    last = nc.scalar.activation(yn_sb[:, u % 2, t], bank[:, Y_BANKS[u % 4], t * P:(t + 1) * P],
                                                ACT.Identity, bias=shift2[:, u, t:t + 1], scale=r2[:, u, t:t + 1])
                last.then_inc(yn_done, 1)

            def normalise3(u):
                act.wait_ge(r2_done, u + XL + 1)
                for t in range(TH):
                    g, c = u + XL, TH + t
                    last = nc.scalar.activation(norm_sb[:, TH * u + t], x_sb[:, TH * u + t], ACT.Identity,
                                                bias=shift2[:, g, c:c + 1], scale=r2[:, g, c:c + 1])
                last.then_inc(h2_done, 1)

            def copy_h2T(u):
                act.wait_ge(t_full, t_at["h2", u] + 1)
                if u >= 2:
                    act.wait_ge(z_full, u - 1)
                nc.scalar.copy(h2T[:, u % 2], t_bank(("h2", u))).then_inc(t_free, 1)

            def gelu(u):
                act.wait_ge(z_full, u + 1)
                act.wait_ge(s_col_done, u + 1)
                nc.scalar.activation(g_sb[:, TH * u:TH * u + TH].rearrange("p (a t) d -> p a t d", a=2),
                                     z_ps()[:, :, :, 0:P], ACT.Gelu_apprx_tanh).then_inc(gelu_done, 1)

            def copy_s_row(u):
                b = u // 2
                act.wait_ge(t_full, t_at["s", u] + 1)
                if b >= 2:
                    act.wait_ge(beats_done, b - 1)
                a = HW * (u % 2)
                nc.scalar.copy(s_row[:, b % 2, a:a + HW], t_bank(("s", u))).then_inc(t_free, 1)

            def copy_rank(b):
                act.wait_ge(t_full, t_at["r", b] + 1)
                if b >= 2:
                    act.wait_ge(dropped_done, b - 1)
                nc.scalar.copy(rank_sb[:, b % 2], t_bank(("r", b))[:, 0:T]).then_inc(t_free, 1)

            normalise1(0)
            for i in range(ROUNDS):
                s = i - OFF
                if i < U:
                    copy_hT(i)
                if 1 <= i <= U:
                    exp_q_half(i - 1)
                if i % 2 and (i + 1) // 2 < B:
                    normalise1((i + 1) // 2)
                if 1 <= i <= U:
                    exp_k_half(i - 1)
                if i >= 4 and i % 2 == 0 and (i - 4) // 2 < B:
                    seed_norms((i - 4) // 2)
                if i >= VKL and (i - VKL) % 2 == 0 and (i - VKL) // 2 < B:
                    copy_M((i - VKL) // 2)
                if 2 <= i < U + 2:
                    square_k(i - 2)
                if 1 <= i <= U:
                    copy_v(i - 1)
                if XL + 2 <= s < U + XL + 2:
                    copy_s_row(s - XL - 2)
                if XL + 1 <= s < U + XL + 1:
                    copy_h2T(s - XL - 1)
                if s >= RL and (s - RL) % 2 == 0 and (s - RL) // 2 < B:
                    copy_rank((s - RL) // 2)
                if 0 <= s < U:
                    y_norm(s)
                if XL <= s < U + XL:
                    normalise3(s - XL)
                if XL + 1 <= s < U + XL + 1:
                    gelu(s - XL - 1)

        @block.vector
        def _(dve):
            chain = [0]

            def link(ins):
                chain[0] += 1
                ins.then_inc(dve_chain, 1)
                dve.wait_ge(dve_chain, chain[0])

            nc.vector.memset(ones_col[:], 1.0)
            nc.vector.memset(ones3[:], 1.0)
            nc.vector.memset(minus1[:], -1.0).then_inc(dve_const, 1)

            nc.vector.memset(eps1[:], LN_EPS)
            nc.vector.memset(eps2[:, 0:TH], ATTN_EPS)
            link(nc.vector.memset(eps2[:, TH:T], LN_EPS))

            rstd_at = [0]
            RSTD_STEPS = 13

            def rstd(n, mean, m2, eps, v, y, t, i, r, shift):
                if n:
                    dve.wait_ge(rstd_step, rstd_at[0])
                if n == 0:
                    ins = nc.vector.scalar_tensor_tensor(out=v, in0=m2, scalar=1.0 / D, in1=eps, op0=ALU.mult, op1=ALU.add)
                elif n == 1:
                    ins = nc.vector.tensor_scalar(i, v.bitcast(I32), 1, None, ALU.logical_shift_right)
                elif n == 2:
                    ins = nc.vector.tensor_scalar(y.bitcast(I32), i, -1.0, float(0x5f3759df), ALU.mult, ALU.add)
                elif n == RSTD_STEPS - 1:
                    ins = nc.vector.scalar_tensor_tensor(out=shift, in0=mean, scalar=-1.0, in1=r, op0=ALU.mult, op1=ALU.mult)
                elif n % 3 == 0:
                    ins = nc.vector.tensor_tensor(t, y, y, ALU.mult)
                elif n % 3 == 1:
                    ins = nc.vector.scalar_tensor_tensor(out=t, in0=t, scalar=-0.5, in1=v, op0=ALU.mult, op1=ALU.mult)
                else:
                    ins = nc.vector.scalar_tensor_tensor(out=r if n == RSTD_STEPS - 2 else y, in0=t, scalar=1.5, in1=y,
                                                         op0=ALU.add, op1=ALU.mult)
                if n < RSTD_STEPS - 1:
                    rstd_at[0] += 1
                    ins.then_inc(rstd_step, 1)
                return ins

            def bn_x(b, g):
                if g % 2 == 0:
                    dve.wait_ge(x_in[2 * b + g // 2], 16)
                return nc.vector.bn_stats(bn1[:, b, g, :], pairs(x_sb, T // 2 * b + g))

            def rstd1(n, b0, b1):
                v = bn1[:, b0:b1].rearrange("p b g (e s) -> p b (g e) s", s=3)
                cols = (a[:, b0:b1] for a in (eps1, var1, root1, root1b, bits1, r1, shift1))
                return rstd(n, v[:, :, :, 1], v[:, :, :, 2], *cols)

            def bias_step(n):
                if n == 0:
                    dve.wait_ge(bias_in, 16 * 4)
                    dve.wait_ge(later_set, 1)
                else:
                    dve.wait_ge(dve_chain, chain[0])
                if n == 0:
                    ins = nc.vector.tensor_scalar(bias_f[:, 0:2 * P], bias_f[:, 0:2 * P], 1.0, None, ALU.add)
                elif n == 5:
                    nc.vector.tensor_copy(bias3[:], bias_f[:]).then_inc(bias_set, 1)
                    return
                elif n % 2:
                    ins = nc.vector.tensor_copy(bias_cut[:], bias_f[:])
                else:
                    ins = nc.vector.scalar_tensor_tensor(out=bias_f[:], in0=bias_cut[:],
                                                         scalar=minus_later[:, n // 2 - 1:n // 2], in1=bias_f[:],
                                                         op0=ALU.mult, op1=ALU.add)
                chain[0] += 1
                ins.then_inc(dve_chain, 1)

            def normalise1(b):
                dve.wait_ge(r1_done, 1 if b == 0 else 2)
                mean, _ = stats(bn1, b)
                for t in range(TH):
                    last = nc.vector.tensor_scalar(norm_sb[:, T * b + t], x_sb[:, T * b + t], mean[:, t:t + 1],
                                                   r1[:, b, t:t + 1], ALU.subtract, ALU.mult)
                last.then_inc(h_done, 1)

            def q_half(u):
                dve.wait_ge(expq_done, u + 1)
                nc.vector.scalar_tensor_tensor(out=qT[:, u], in0=exp_q[:, u % 2], scalar=1.0,
                                               in1=bank[:, Q_BANKS[u % 2], :], op0=ALU.min, op1=ALU.max).then_inc(q_done, 1)

            def k_half(u):
                dve.wait_ge(expk_done, u + 1)
                nc.vector.scalar_tensor_tensor(out=k_sb[:, u],
                                               in0=exp_k[:, u % 2].rearrange("p (t d) -> p t d", d=D), scalar=1.0,
                                               in1=kv_ps(u)[:, :, 0:P], op0=ALU.min, op1=ALU.max).then_inc(k_done, 1)

            def key_norms(b):
                dve.wait_ge(seed_done, b + 1)
                if b:
                    dve.wait_ge(kn_done, b)
                r, n = k_seed[:, b % 2], k_ssq[:, b % 2]
                link(nc.vector.tensor_tensor(k_tmp[:], r, r, ALU.mult))
                link(nc.vector.scalar_tensor_tensor(out=k_tmp[:], in0=k_tmp[:], scalar=-0.5, in1=n, op0=ALU.mult, op1=ALU.mult))
                nc.vector.scalar_tensor_tensor(out=k_rnorm[:], in0=k_tmp[:], scalar=1.5, in1=r, op0=ALU.add,
                                               op1=ALU.mult).then_inc(rnorm_done, 1)
                dve.wait_ge(rnorm_done, b + 1)
                k = k_sb[:, 2 * b:2 * b + 2].rearrange("p u t (h e) -> p (u t h) e", e=DEPTH)
                nc.vector.tensor_tensor(k, k, k_rnorm[:].unsqueeze(2).to_broadcast([P, T * HEADS, DEPTH]),
                                        ALU.mult).then_inc(kn_done, 1)

            def mask_vk(b):
                if b == 0:
                    dve.wait_ge(mask_set, 1)
                dve.wait_ge(vk_full, b + 1)
                nc.vector.tensor_tensor(vk_sb[:, b % 2], t_bank(("M", b))[:, 0:P], head_mask[:], ALU.mult).then_inc(vk_done, 1)

            def row_stats(s):
                if s < U:
                    dve.wait_ge(y_full, s + 1)
                    y = bank[:, Y_BANKS[s % 4], :].rearrange("p (t d) -> p t d", d=D)
                    for g in range(TH // 2):
                        last = nc.vector.bn_stats(bn2[:, s, g, :], pairs(y, g))
                if s >= XL:
                    u = s - XL
                    dve.wait_ge(x1_done, u + 1)
                    for g in range(TH // 2):
                        last = nc.vector.bn_stats(bn2[:, s, TH // 2 + g, :], pairs(x_sb, TH // 2 * u + g))
                link(last)

            def rstd2(n, s):
                c0, c1 = 0 if s < U else TH, T if s >= XL else TH
                ins = rstd(n, *(a[:, c0:c1] for a in (*stats(bn2, s), eps2, var, root, root2, bits, r2[:, s], shift2[:, s])))
                if n == RSTD_STEPS - 1:
                    ins.then_inc(r2_done, 1)

            def score_cols(u):
                dve.wait_ge(z_full, u + 1)
                nc.vector.tensor_copy(s_col[:, TH * u:TH * u + TH].rearrange("p (a t) -> p a t", a=2),
                                      z_ps()[:, :, :, P]).then_inc(s_col_done, 1)

            def compare(b, n):
                s, J, part = b % 2, n // 3, n % 3
                if n == 0:
                    dve.wait_ge(t_free, t_at["s", 2 * b + 1] + 1)
                    if b == 0:
                        dve.wait_ge(lower_set, 1)
                    if b >= 2:
                        dve.wait_ge(t_full, t_at["r", b - 2] + 1)
                s_j = s_col[:, T * b + J:T * b + J + 1]
                a = P * (J + 1)
                if part == 0:
                    nc.vector.tensor_scalar(beats[:, s, J, 0:a], s_row[:, s, 0:a], s_j, None, ALU.is_lt)
                elif part == 1 and J < T - 1:
                    nc.vector.tensor_scalar(beats[:, s, J, a:], s_row[:, s, a:], s_j, None, ALU.is_le)
                elif part == 2:
                    last = nc.vector.scalar_tensor_tensor(out=ties[:, s, J], in0=s_row[:, s, P * J:a], scalar=s_j,
                                                          in1=lower[:], op0=ALU.is_equal, op1=ALU.mult)
                    if J == T - 1:
                        last.then_inc(beats_done, 1)

            def merge(b):
                dve.wait_ge(t_free, t_at["r", b] + 1)
                nc.vector.tensor_scalar(dropped[:, b % 2], rank_sb[:, b % 2], KEEP - 0.5, None, ALU.is_gt).then_inc(dropped_done, 1)
                dve.wait_ge(dropped_done, b + 1)
                dve.wait_ge(gelu_done, 2 * b + 2)
                nc.vector.copy_predicated(g_sb[:, T * b:T * (b + 1)],
                                          dropped[:, b % 2].unsqueeze(2).to_broadcast([P, T, D]),
                                          norm_sb[:, T * b:T * (b + 1)]).then_inc(merged, 1)

            for g in range(T // 2):
                last = bn_x(0, g)
            link(last)
            for n in range(RSTD_STEPS):
                last = rstd1(n, 0, 1)
                if n < 4:
                    bn_x(1, n)
                elif n < 10:
                    bias_step(n - 4)
            last.then_inc(r1_done, 1)
            normalise1(0)
            for b in range(2, B):
                for g in range(T // 2):
                    last = bn_x(b, g)
            link(last)
            for n in range(RSTD_STEPS):
                last = rstd1(n, 1, B)
            last.then_inc(r1_done, 1)
            normalise1(1)
            for i in range(1, ROUNDS):
                s = i - OFF
                if i <= U:
                    q_half(i - 1)
                if i >= VKL and (i - VKL) % 2 == 0 and (i - VKL) // 2 < B:
                    mask_vk((i - VKL) // 2)
                if i <= U:
                    k_half(i - 1)
                if i % 2 == 0 and i + 2 < U:
                    normalise1((i + 2) // 2)
                if i >= 5 and i % 2 and (i - 5) // 2 < B:
                    key_norms((i - 5) // 2)
                if 0 <= s < U + XL:
                    row_stats(s)
                c = s - CL
                for n in range(RSTD_STEPS):
                    if 0 <= s < U + XL:
                        rstd2(n, s)
                    if n < 12 and 0 <= c < U:
                        compare(c // 2, 12 * (c % 2) + n)
                if XL + 1 <= s < U + XL + 1:
                    score_cols(s - XL - 1)
                if s >= RL and (s - RL) % 2 == 0 and (s - RL) // 2 < B:
                    merge((s - RL) // 2)

        @block.tensor
        def _(pe):
            def take_t(use):
                if t_at[use] >= 2:
                    pe.wait_ge(t_free, t_at[use] - 1)

            def transpose_h(u):
                pe.wait_ge(h_done_act if u % 2 else h_done, u // 2 + 1)
                if u == 0:
                    pe.wait_ge(ident_set, 1)
                take_t(("h", u))
                for t in range(TH):
                    last = nc.tensor.transpose(t_bank(("h", u))[:, t * P:(t + 1) * P], norm_sb[:, TH * u + t], ident[:])
                last.then_inc(t_full, 1)

            def q_proj(u):
                pe.wait_ge(t_free, t_at["h", u] + 1)
                if u == 0:
                    pe.wait_ge(wq_in, 16)
                    pe.wait_ge(bias_set, 1)
                    pe.wait_ge(dve_const, 1)
                if u >= 2:
                    pe.wait_ge(q_done, u - 1)
                o = bank[:, Q_BANKS[u % 2], :]
                nc.tensor.matmul(o, wq_sb[:], hT[:, u], start=True, stop=False)
                nc.tensor.matmul(o, bias3[:, 0:P], ones3[:], start=False, stop=True).then_inc(q_full, 1)

            def kv_proj(u):
                if u == 0:
                    pe.wait_ge(wkv_in, 32)
                if u >= 2:
                    pe.wait_ge(v_done, u - 1)
                for t in range(TH):
                    o = kv_ps(u)[:, t, :]
                    nc.tensor.matmul(o, hT[:, u, t * P:(t + 1) * P], wkv_sb[:], start=True, stop=False)
                    last = nc.tensor.matmul(o, ones3[:, 0:P], bias3[:, P:3 * P], start=False, stop=True)
                last.then_inc(kv_full, 1)

            def attention_matrix(b):
                pe.wait_ge(kn_done, b + 1)
                pe.wait_ge(v_done, 2 * b + 2)
                take_t(("M", b))
                o = t_bank(("M", b))
                for t in range(T):
                    u = 2 * b + t // TH
                    last = nc.tensor.matmul(o[:, 0:P], v_sb[:, u, t % TH], k_sb[:, u, t % TH], start=(t == 0), stop=(t == T - 1))
                last.then_inc(vk_full, 1)

            def attention_out(b):
                if b == 0:
                    pe.wait_ge(wo_in, 16)
                pe.wait_ge(vk_done, b + 1)
                nc.tensor.matmul(t_bank(("M", b))[:, P:2 * P], vk_sb[:, b % 2], wo_sb[:], start=True, stop=True).then_inc(t_full, 1)

            def y_half(u):
                b = u // 2
                pe.wait_ge(t_free, t_at["M", b] + 1)
                pe.wait_ge(q_done, U)
                if u >= 4:
                    pe.wait_ge(yn_done, u - 3)
                elif u >= 2:
                    pe.wait_ge(v_done, U)
                for t in range(TH):
                    o = bank[:, Y_BANKS[u % 4], t * P:(t + 1) * P]
                    nc.tensor.matmul(o, qT[:, u, t * P:(t + 1) * P], M_sb[:, b], start=True, stop=False)
                    nc.tensor.matmul(o, hT[:, u, t * P:(t + 1) * P], ident[:], start=False, stop=False)
                    last = nc.tensor.matmul(o, ones3[:, 0:P], bias3[:, 3 * P:4 * P], start=False, stop=True)
                last.then_inc(y_full, 1)

            def transpose_h2(u):
                pe.wait_ge(h2_done, u + 1)
                take_t(("h2", u))
                for t in range(TH):
                    last = nc.tensor.transpose(t_bank(("h2", u))[:, t * P:(t + 1) * P], norm_sb[:, TH * u + t], ident[:])
                last.then_inc(t_full, 1)

            def z_half(u):
                pe.wait_ge(t_free, t_at["h2", u] + 1)
                if u == 0:
                    pe.wait_ge(wz_in, 32)
                    pe.wait_ge(v_done, U)
                if u >= 1:
                    pe.wait_ge(gelu_done, u)
                    pe.wait_ge(s_col_done, u)
                for t in range(TH):
                    last = nc.tensor.matmul(z_ps()[:, t // 2, t % 2, :], h2T[:, u % 2, t * P:(t + 1) * P], wz_sb[:],
                                            start=True, stop=True)
                last.then_inc(z_full, 1)

            def score_rows(u):
                pe.wait_ge(s_col_done, u + 1)
                take_t(("s", u))
                for t in range(TH):
                    n = TH * u + t
                    last = nc.tensor.transpose(t_bank(("s", u))[:, t * P:(t + 1) * P],
                                               s_col[:, n:n + 1].to_broadcast([P, P]), ident[:])
                last.then_inc(t_full, 1)

            def rank(b):
                s = b % 2
                pe.wait_ge(beats_done, b + 1)
                take_t(("r", b))
                o = t_bank(("r", b))
                for i in range(T):
                    for J in range(T):
                        nc.tensor.matmul(o[:, i:i + 1], beats[:, s, J, i * P:(i + 1) * P], ones_col[:],
                                         start=(J == 0), stop=False)
                    last = nc.tensor.matmul(o[:, i:i + 1], ties[:, s, i], ones_col[:], start=False, stop=True)
                last.then_inc(t_full, 1)

            for i in range(ROUNDS):
                s = i - OFF
                if i < U:
                    transpose_h(i)
                if i >= VKL and (i - VKL) % 2 == 0 and (i - VKL) // 2 < B:
                    attention_matrix((i - VKL) // 2)
                if 1 <= i <= U:
                    q_proj(i - 1)
                if i >= VKL and (i - VKL) % 2 == 0 and (i - VKL) // 2 < B:
                    attention_out((i - VKL) // 2)
                if 1 <= i <= U:
                    kv_proj(i - 1)
                if 0 <= s + 1 < U:
                    y_half(s + 1)
                if XL + 2 <= s < U + XL + 2:
                    score_rows(s - XL - 2)
                if XL + 1 <= s < U + XL + 1:
                    transpose_h2(s - XL - 1)
                if s >= RL and (s - RL) % 2 == 0 and (s - RL) // 2 < B:
                    rank((s - RL) // 2)
                if XL + 1 <= s < U + XL + 1:
                    z_half(s - XL - 1)


_INS = ['L0_attn_x', 'L0_attn_Wq', 'L0_attn_bq', 'L0_attn_Wk', 'L0_attn_bk', 'L0_attn_Wv', 'L0_attn_bv', 'L0_attn_Wo',
        'L0_attn_bo', 'L0_attn_gamma', 'L0_attn_beta', 'L0_ffn_w_router', 'L0_ffn_w_block']
_OUTS = [((4, 1024, 128), 'float32')]


def kernel(**inputs):
    import numpy as _np
    import concourse.bacc as _bacc
    from concourse import mybir as _mybir
    from concourse.bass_utils import run_bass_kernel_spmd as _run

    nc = _bacc.Bacc("TRN2", target_bir_lowering=False, num_devices=1)
    arrays, args = {}, []
    for name in _INS:
        a = _np.ascontiguousarray(inputs[name])
        arrays[f"in_{name}_dram"] = a
        args.append(nc.dram_tensor(f"in_{name}_dram", a.shape, _mybir.dt.from_np(a.dtype), kind="ExternalInput").ap())
    for i, (shape, dtype) in enumerate(_OUTS):
        dt = _mybir.dt.from_np(_np.dtype(dtype))
        args.append(nc.dram_tensor(f"out_{i}_dram", shape, dt, kind="ExternalOutput").ap())
    preln_linear_attention_mod_ffn(nc, *args)
    r = _run(nc, [arrays], core_ids=[0])
    got = tuple(r.results[0][f"out_{i}_dram"] for i in range(len(_OUTS)))
    return got[0]
```

```python
from contextlib import ExitStack

import concourse.bass as bass
from concourse import mybir

ALU = mybir.AluOpType
ACT = mybir.ActivationFunctionType
F32 = mybir.dt.float32
BF16 = mybir.dt.bfloat16
I32 = mybir.dt.int32

P = 128
HEADS, DEPTH = 16, 8
LN_EPS = 1e-5
ATTN_EPS = 1e-6
CAPACITY = 0.75
TH = 4


def preln_linear_attention_mod_ffn(nc, x, wq, bq, wk, bk, wv, bv, wo, bo, gamma, beta, w_router, w_block, out):
    B, L, D = x.shape
    assert D == P and HEADS * DEPTH == D and L % (2 * TH * P) == 0
    T = L // P
    U = B * T // TH
    HW = TH * P
    KEEP = max(1, int(L * CAPACITY))
    assert T == 2 * TH
    KRING = 6
    XL = 2
    Y_BANKS = (3, 3, 2, 5, 4, 3, 4, 3)

    early = [("equal", 0, 0, HW)] + [("le", J, P * J, HW) for J in range(TH)]
    late = [("equal", TH, HW, 2 * HW)] + [("le", J, max(P * J, HW), 2 * HW) for J in range(T)]
    PIECES = len(early) + len(late)

    x_v = x.rearrange("b (t p) d -> b p t d", p=P)
    out_v = out.rearrange("b (t p) d -> b p t d", p=P)

    with ExitStack() as ctx:
        def sb(name, shape, dt=F32):
            return ctx.enter_context(nc.sbuf_tensor(name, shape, dt))

        def sem(name):
            return ctx.enter_context(nc.semaphore(name))

        x_sb = sb("x_sb", [P, B * T, D])
        norm_sb = sb("norm_sb", [P, B * T, D])
        hT = sb("hT", [P, U, HW])
        qT = sb("qT", [P, U, HW])
        exp_q = sb("exp_q", [P, 2, HW])
        exp_k = sb("exp_k", [P, 2, HW])
        k_sb = sb("k_sb", [P, KRING, TH, D])
        k2_sb = sb("k2_sb", [P, 2, TH * HEADS, DEPTH])
        k_add4 = sb("k_add4", [P, 2, TH * HEADS, 4])
        k_add2 = sb("k_add2", [P, 2, TH * HEADS, 2])
        k_ssq = sb("k_ssq", [P, 2, T * HEADS])
        k_seed = sb("k_seed", [P, 2, T * HEADS])
        k_tmp = sb("k_tmp", [P, T * HEADS])
        k_rnorm = sb("k_rnorm", [P, T * HEADS])
        v_sb = sb("v_sb", [P, KRING, TH, D])
        vk_sb = sb("vk_sb", [P, 2, P])
        M_sb = sb("M_sb", [P, B, P])
        yn_sb = sb("yn_sb", [P, 2, TH, D])
        h2T = sb("h2T", [P, 2, HW])
        g_sb = sb("g_sb", [P, B * T, D])
        s_col = sb("s_col", [P, B * T])
        s_row = sb("s_row", [P, B, T * P])
        beats = sb("beats", [P, 2, T, T * P], BF16)
        ties = sb("ties", [P, 2, T, P], BF16)
        rank_sb = sb("rank_sb", [P, 2, 2 * T])
        part_sums = sb("part_sums", [P, T * P], BF16)
        ident16 = sb("ident16", [P, P], BF16)
        ones16 = sb("ones16", [P, P], BF16)
        later_tiles = sb("later_tiles", [P, T], BF16)
        dropped = sb("dropped", [P, 2, T], I32)
        bn1 = sb("bn1", [P, B, T // 2, 6])
        bn2 = sb("bn2", [P, U + XL, T // 2, 6])
        r1 = sb("r1", [P, B, T])
        var1, root1, root1b = sb("var1", [P, B, T]), sb("root1", [P, B, T]), sb("root1b", [P, B, T])
        bits1 = sb("bits1", [P, B, T], I32)
        shift1 = sb("shift1", [P, B, T])
        r2 = sb("r2", [P, U + XL, T])
        shift2 = sb("shift2", [P, U + XL, T])
        var = sb("var", [P, T])
        root = sb("root", [P, T])
        root2 = sb("root2", [P, T])
        bits = sb("bits", [P, T], I32)
        eps1 = sb("eps1", [P, B, T])
        eps2 = sb("eps2", [P, T])
        ident = sb("ident", [P, P])
        lower = sb("lower", [P, P])
        head_mask = sb("head_mask", [P, P])
        minus1 = sb("minus1", [P, 1])
        ones3 = sb("ones3", [3, HW], BF16)
        wq_sb = sb("wq_sb", [P, P])
        wkv_sb = sb("wkv_sb", [P, 2 * P])
        wo_sb = sb("wo_sb", [P, P])
        wz_sb = sb("wz_sb", [P, P + 1])
        gamma_sb = sb("gamma_sb", [P, P])
        beta_sb = sb("beta_sb", [P, P])
        bias_f = sb("bias_f", [3, 4 * P])
        bias_cut = sb("bias_cut", [3, 4 * P], BF16)
        minus_later = sb("minus_later", [3, 2])
        bias3 = sb("bias3", [3, 4 * P], BF16)

        bank = ctx.enter_context(nc.psum_tensor("bank", [P, 8, HW], F32))
        Q_BANK = 2

        def kv_ps(u):
            a = 4 + 2 * (u % 2)
            return bank[:, a:a + 2, :].rearrange("p a (t c) -> p (a t) c", c=2 * P)

        def z_ps():
            return bank[:, 6:8, 0:2 * (P + 1)].rearrange("p a (t c) -> p a t c", c=P + 1)

        x_in = [sem(f"x_in{b}") for b in range(2 * B)]
        wq_in, wkv_in, wo_in, wz_in = sem("wq_in"), sem("wkv_in"), sem("wo_in"), sem("wz_in")
        bias_in, gb_in = sem("bias_in"), sem("gb_in")
        out_stored = sem("out_stored")
        pool_chain = sem("pool_chain")
        dve_chain = sem("dve_chain")
        ident_set, lower_set, mask_set = sem("ident_set"), sem("lower_set"), sem("mask_set")
        dve_const, bias_set = sem("dve_const"), sem("bias_set")
        r1_done, h_done, h_done_act = sem("r1_done"), sem("h_done"), sem("h_done_act")
        t_fulls, t_frees = (sem("t0_full"), sem("t1_full")), (sem("t0_free"), sem("t1_free"))
        vk_full, vk_done = sem("vk_full"), sem("vk_done")
        q_full, expq_done, q_done = sem("q_full"), sem("expq_done"), sem("q_done")
        kv_full, expk_done, k_done, k2_done = sem("kv_full"), sem("expk_done"), sem("k_done"), sem("k2_done")
        rnorm_done, kn_done, v_done = sem("rnorm_done"), sem("kn_done"), sem("v_done")
        xb_done = sem("xb_done")
        var_done, root_done, lnv_done = sem("var_done"), sem("root_done"), sem("lnv_done")
        ssq_done, seed_done, ln_done = sem("ssq_done"), sem("seed_done"), sem("ln_done")
        rstd_step, later_set = sem("rstd_step"), sem("later_set")
        y_full, r2_done, yn_done = sem("y_full"), sem("r2_done"), sem("yn_done")
        x1_done, h2_done = sem("x1_done"), sem("h2_done")
        z_full, gelu_done, s_col_done = sem("z_full"), sem("gelu_done"), sem("s_col_done")
        beats_done, equal_done, ties_done = sem("beats_done"), sem("equal_done"), sem("ties_done")
        dropped_done, merged, gelu_sums, norm_sums = sem("dropped_done"), sem("merged"), sem("gelu_sums"), sem("norm_sums")

        T_USES = (
            (("h", 0), ("h", 1), ("h", 2), ("h", 3), ("h", 4), ("h", 5), ("h", 6), ("h", 7), ("h2", 0),
             ("h2", 1), ("h2", 2), ("h2", 3), ("h2", 4), ("h2", 5), ("tb", 0), ("h2", 6), ("h2", 7), ("tb", 1),
             ("tb", 2), ("tb", 3),),
            (("M", 0), ("M", 1), ("M", 2), ("M", 3), ("s", 0), ("s", 1), ("s", 2), ("s", 3), ("ta", 0),
             ("s", 4), ("r", 0), ("s", 5), ("ta", 1), ("s", 6), ("r", 1), ("s", 7), ("ta", 2), ("r", 2),
             ("ta", 3), ("r", 3),))
        t_at = {use: at for uses in T_USES for at, use in enumerate(uses)}
        BANK_OF = {"h": 0, "h2": 0, "tb": 0, "M": 1, "s": 1, "ta": 1, "r": 1}

        def t_bank(use):
            return bank[:, BANK_OF[use[0]], :]

        def stats(bn, group):
            v = bn[:, group].rearrange("p g (e s) -> p (g e) s", s=3)
            return v[:, :, 1], v[:, :, 2]

        def pairs(ap, g):
            return ap[:, 2 * g:2 * g + 2, :].rearrange("p t d -> p d t")

        block = ctx.enter_context(nc.Block())

        @block.sync
        def _(sp):
            for u in range(U):
                b, a = u // 2, TH * (u % 2)
                if u != 1:
                    sp.dma_start(x_sb[:, TH * u:TH * u + TH, :], x_v[b, :, a:a + TH, :]).then_inc(x_in[u], 16)
                if u == 0:
                    sp.dma_start(wq_sb[:], wq).then_inc(wq_in, 16)
                    sp.dma_start(wkv_sb[:, 0:P], wk).then_inc(wkv_in, 16)
                    sp.dma_start(wkv_sb[:, P:2 * P], wv).then_inc(wkv_in, 16)
            for u in range(U):
                sp.wait_ge(merged, u + 1)
                b, a = u // 2, TH * (u % 2)
                sp.dma_start(out_v[b, :, a:a + TH, :], g_sb[:, TH * u:TH * u + TH, :]).then_inc(out_stored, 16)
            sp.wait_ge(out_stored, 16 * U)

        @block.gpsimd
        def _(pool):
            chain = [0]

            def link(ins):
                chain[0] += 1
                ins.then_inc(pool_chain, 1)
                pool.wait_ge(pool_chain, chain[0])

            for n, vec in enumerate((bq, bk, bv, bo)):
                pool.dma_start(bias_f[:, n * P:(n + 1) * P], vec.partition_broadcast(3)).then_inc(bias_in, 16)
            link(nc.gpsimd.memset(ident[:], 0.0))
            nc.gpsimd.affine_select(out=ident[:], in_=ident[:], compare_op=ALU.not_equal, fill=1.0, base=0,
                                    pattern=[[-1, P]], channel_multiplier=1).then_inc(ident_set, 1)
            link(nc.gpsimd.memset(minus_later[:], -1.0))
            nc.gpsimd.affine_select(out=minus_later[:], in_=minus_later[:], compare_op=ALU.is_ge, fill=0.0, base=-1,
                                    pattern=[[-1, 2]], channel_multiplier=1).then_inc(later_set, 1)

            def masks():
                for J in range(T):
                    nc.gpsimd.memset(later_tiles[:, J:J + 1], float(T - J))
                nc.gpsimd.memset(ones16[:], 1.0)
                link(nc.gpsimd.memset(ident16[:], 0.0))
                link(nc.gpsimd.affine_select(out=ident16[:], in_=ident16[:], compare_op=ALU.not_equal, fill=1.0, base=0,
                                             pattern=[[-1, P]], channel_multiplier=1))
                link(nc.gpsimd.memset(lower[:], 1.0))
                nc.gpsimd.affine_select(out=lower[:], in_=lower[:], compare_op=ALU.is_gt, fill=0.0, base=0,
                                        pattern=[[1, P]], channel_multiplier=-1).then_inc(lower_set, 1)
                link(nc.gpsimd.memset(head_mask[:], 1.0))
                link(nc.gpsimd.affine_select(out=head_mask[:], in_=head_mask[:], compare_op=ALU.is_ge, fill=0.0, base=0,
                                             pattern=[[-DEPTH, HEADS], [0, DEPTH]], channel_multiplier=1))
                nc.gpsimd.affine_select(out=head_mask[:], in_=head_mask[:], compare_op=ALU.is_ge, fill=0.0,
                                        base=DEPTH - 1, pattern=[[DEPTH, HEADS], [0, DEPTH]],
                                        channel_multiplier=-1).then_inc(mask_set, 1)

            def key_sums(u):
                s, b = u % 2, u // 2
                pool.wait_ge(k2_done, u + 1)
                k2 = k2_sb[:, s]
                o = k_ssq[:, b % 2, s * TH * HEADS:(s + 1) * TH * HEADS]
                link(nc.gpsimd.tensor_tensor(k_add4[:, s], k2[:, :, 0:4], k2[:, :, 4:8], ALU.add))
                link(nc.gpsimd.tensor_tensor(k_add2[:, s], k_add4[:, s, :, 0:2], k_add4[:, s, :, 2:4], ALU.add))
                if u % 2 == 0 and b >= 2:
                    pool.wait_ge(rnorm_done, b - 1)
                link(nc.gpsimd.tensor_tensor(o, k_add2[:, s, :, 0], k_add2[:, s, :, 1], ALU.add))
                nc.gpsimd.tensor_scalar(o, o, 1.0, ATTN_EPS, ALU.mult, ALU.add).then_inc(ssq_done, 1)

            def add_beta(u):
                pool.wait_ge(h_done_act if u % 2 else h_done, u // 2 + 1)
                if u == 0:
                    pool.wait_ge(gb_in, 32)
                a = TH * u
                nc.gpsimd.tensor_tensor(x_sb[:, a:a + TH], x_sb[:, a:a + TH],
                                        beta_sb[:].unsqueeze(1).to_broadcast([P, TH, D]), ALU.add).then_inc(xb_done, 1)

            def residual(u):
                a = TH * u
                pool.wait_ge(yn_done, u + 1)
                link(nc.gpsimd.tensor_tensor(yn_sb[:, u % 2], yn_sb[:, u % 2],
                                             gamma_sb[:].unsqueeze(1).to_broadcast([P, TH, D]), ALU.mult))
                pool.wait_ge(xb_done, u + 1)
                nc.gpsimd.tensor_tensor(x_sb[:, a:a + TH], x_sb[:, a:a + TH], yn_sb[:, u % 2],
                                        ALU.add).then_inc(x1_done, 1)

            def mask_ties(u):
                if u == 0:
                    pool.wait_ge(lower_set, 1)
                pool.wait_ge(equal_done, u + 1)
                a = TH * (u % 2)
                t = ties[:, u // 2 % 2, a:a + TH]
                nc.gpsimd.tensor_tensor(t, t, lower[:].unsqueeze(1).to_broadcast([P, TH, P]), ALU.mult).then_inc(ties_done, 1)

            def gelu_sum(u):
                a = TH * u
                pool.wait_ge(gelu_done, u + 1)
                nc.gpsimd.tensor_tensor(g_sb[:, a:a + TH], g_sb[:, a:a + TH], x_sb[:, a:a + TH],
                                        ALU.add).then_inc(gelu_sums, 1)

            def norm_sum(u):
                a = TH * u
                pool.wait_ge(t_fulls[0], t_at["h2", u] + 1)
                nc.gpsimd.tensor_tensor(norm_sb[:, a:a + TH], norm_sb[:, a:a + TH], x_sb[:, a:a + TH],
                                        ALU.add).then_inc(norm_sums, 1)

            masks()
            key_sums(0)
            key_sums(1)
            add_beta(0)
            add_beta(1)
            add_beta(2)
            add_beta(3)
            add_beta(4)
            add_beta(5)
            key_sums(2)
            key_sums(3)
            key_sums(4)
            key_sums(5)
            residual(0)
            key_sums(6)
            key_sums(7)
            residual(1)
            residual(2)
            add_beta(6)
            add_beta(7)
            norm_sum(0)
            residual(3)
            norm_sum(1)
            residual(4)
            gelu_sum(0)
            residual(5)
            norm_sum(2)
            residual(6)
            norm_sum(3)
            gelu_sum(1)
            residual(7)
            mask_ties(0)
            norm_sum(4)
            mask_ties(1)
            mask_ties(2)
            gelu_sum(2)
            gelu_sum(3)
            mask_ties(3)
            mask_ties(4)
            norm_sum(5)
            mask_ties(5)
            norm_sum(6)
            norm_sum(7)
            gelu_sum(4)
            mask_ties(6)
            mask_ties(7)
            gelu_sum(5)
            gelu_sum(6)
            gelu_sum(7)

        @block.scalar
        def _(act):
            nc.scalar.preload_act_table_set("natural_log_exp_and_others")
            act.dma_start(x_sb[:, TH:T, :], x_v[0, :, TH:T, :]).then_inc(x_in[1], 16)
            act.dma_start(beta_sb[:], beta.partition_broadcast(P)).then_inc(gb_in, 16)
            act.dma_start(gamma_sb[:], gamma.partition_broadcast(P)).then_inc(gb_in, 16)
            act.dma_start(wo_sb[:], wo).then_inc(wo_in, 16)
            act.dma_start(wz_sb[:, 0:P], w_block).then_inc(wz_in, 16)
            act.dma_start(wz_sb[:, P:P + 1], w_router.unsqueeze(1)).then_inc(wz_in, 16)

            def normalise1(b):
                act.wait_ge(r1_done, min(b + 1, 3))
                for t in range(TH, T):
                    last = nc.scalar.activation(norm_sb[:, T * b + t], x_sb[:, T * b + t], ACT.Identity,
                                                bias=shift1[:, b, t:t + 1], scale=r1[:, b, t:t + 1])
                last.then_inc(h_done_act, 1)

            def copy_hT(u):
                act.wait_ge(t_fulls[BANK_OF["h"]], t_at["h", u] + 1)
                nc.scalar.copy(hT[:, u], t_bank(("h", u))).then_inc(t_frees[0], 1)

            def exp_q_half(u):
                act.wait_ge(q_full, u + 1)
                if u == 0:
                    act.wait_ge(dve_const, 1)
                if u >= 2:
                    act.wait_ge(q_done, u - 1)
                nc.scalar.activation(exp_q[:, u % 2], bank[:, Q_BANK, :], ACT.Exp,
                                     bias=minus1[:, 0:1]).then_inc(expq_done, 1)

            def exp_k_half(u):
                act.wait_ge(kv_full, u + 1)
                if u >= 2:
                    act.wait_ge(k_done, u - 1)
                nc.scalar.activation(exp_k[:, u % 2].rearrange("p (t d) -> p t d", d=D), kv_ps(u)[:, :, 0:P], ACT.Exp,
                                     bias=minus1[:, 0:1]).then_inc(expk_done, 1)

            def copy_v(u):
                act.wait_ge(k_done, u + 1)
                if u >= KRING:
                    act.wait_ge(vk_full, (u - KRING) // 2 + 1)
                nc.scalar.copy(v_sb[:, u % KRING], kv_ps(u)[:, :, P:2 * P]).then_inc(v_done, 1)

            def square_k(u):
                act.wait_ge(k_done, u + 1)
                if u >= 2:
                    act.wait_ge(ssq_done, u - 1)
                nc.scalar.activation(k2_sb[:, u % 2].rearrange("p h e -> p (h e)"),
                                     k_sb[:, u % KRING].rearrange("p t d -> p (t d)"), ACT.Square).then_inc(k2_done, 1)

            def seed_norms(b):
                act.wait_ge(ssq_done, 2 * b + 2)
                if b >= 2:
                    act.wait_ge(rnorm_done, b - 1)
                nc.scalar.activation(k_seed[:, b % 2], k_ssq[:, b % 2], ACT.Ln).then_inc(ln_done, 1)
                act.wait_ge(ln_done, b + 1)
                nc.scalar.activation(k_seed[:, b % 2], k_seed[:, b % 2], ACT.Exp, scale=-0.5).then_inc(seed_done, 1)

            def copy_M(b):
                act.wait_ge(t_fulls[BANK_OF["M"]], t_at["M", b] + 1)
                nc.scalar.copy(M_sb[:, b], t_bank(("M", b))[:, P:2 * P]).then_inc(t_frees[1], 1)

            def y_norm(u):
                act.wait_ge(r2_done, u + 1)
                if u >= 2:
                    act.wait_ge(x1_done, u - 1)
                for t in range(TH):
                    last = nc.scalar.activation(yn_sb[:, u % 2, t], bank[:, Y_BANKS[u], t * P:(t + 1) * P],
                                                ACT.Identity, bias=shift2[:, u, t:t + 1], scale=r2[:, u, t:t + 1])
                last.then_inc(yn_done, 1)

            def normalise3(u):
                act.wait_ge(r2_done, u + XL + 1)
                for t in range(TH):
                    g, c = u + XL, TH + t
                    last = nc.scalar.activation(norm_sb[:, TH * u + t], x_sb[:, TH * u + t], ACT.Identity,
                                                bias=shift2[:, g, c:c + 1], scale=r2[:, g, c:c + 1])
                last.then_inc(h2_done, 1)

            def copy_h2T(u):
                act.wait_ge(t_fulls[BANK_OF["h2"]], t_at["h2", u] + 1)
                if u >= 2:
                    act.wait_ge(z_full, u - 1)
                nc.scalar.copy(h2T[:, u % 2], t_bank(("h2", u))).then_inc(t_frees[0], 1)

            def gelu(u):
                act.wait_ge(z_full, u + 1)
                act.wait_ge(s_col_done, u + 1)
                nc.scalar.activation(g_sb[:, TH * u:TH * u + TH].rearrange("p (a t) d -> p a t d", a=2),
                                     z_ps()[:, :, :, 0:P], ACT.Gelu_apprx_tanh).then_inc(gelu_done, 1)

            def copy_s_row(u):
                act.wait_ge(t_fulls[BANK_OF["s"]], t_at["s", u] + 1)
                a = HW * (u % 2)
                nc.scalar.copy(s_row[:, u // 2, a:a + HW], t_bank(("s", u))).then_inc(t_frees[1], 1)

            def copy_sums(b, half):
                n, use = ((1, "ta"), (0, "tb"))[half]
                act.wait_ge(t_fulls[n], t_at[use, b] + 1)
                if b:
                    act.wait_ge(t_fulls[1], t_at["r", b - 1] + 1)
                nc.scalar.copy(part_sums[:, half * HW:(half + 1) * HW], t_bank((use, b))).then_inc(t_frees[n], 1)

            def copy_rank(b):
                act.wait_ge(t_fulls[BANK_OF["r"]], t_at["r", b] + 1)
                if b >= 2:
                    act.wait_ge(dropped_done, b - 1)
                nc.scalar.copy(rank_sb[:, b % 2], t_bank(("r", b))[:, 0:2 * T]).then_inc(t_frees[1], 1)

            for b in (0, 1):
                act.wait_ge(var_done, b + 1)
                nc.scalar.activation(root1b[:, b], var1[:, b], ACT.Ln).then_inc(lnv_done, 1)
                act.wait_ge(lnv_done, b + 1)
                nc.scalar.activation(root1[:, b], root1b[:, b], ACT.Exp, scale=-0.5).then_inc(root_done, 1)
                if b == 0:
                    normalise1(0)
                    copy_hT(0)
            exp_q_half(0)
            copy_hT(1)
            normalise1(1)
            copy_hT(2)
            exp_k_half(0)
            exp_k_half(1)
            copy_v(0)
            square_k(0)
            copy_hT(3)
            copy_v(1)
            exp_q_half(1)
            square_k(1)
            exp_k_half(2)
            normalise1(2)
            seed_norms(0)
            copy_hT(4)
            copy_v(2)
            exp_k_half(3)
            exp_q_half(2)
            copy_hT(5)
            square_k(2)
            square_k(3)
            copy_v(3)
            normalise1(3)
            exp_k_half(4)
            copy_M(0)
            exp_q_half(3)
            copy_hT(6)
            copy_v(4)
            exp_q_half(4)
            exp_k_half(5)
            seed_norms(1)
            square_k(4)
            square_k(5)
            exp_q_half(5)
            copy_v(5)
            copy_hT(7)
            seed_norms(2)
            exp_q_half(6)
            y_norm(0)
            exp_k_half(6)
            exp_k_half(7)
            copy_v(6)
            square_k(6)
            copy_v(7)
            square_k(7)
            exp_q_half(7)
            copy_M(1)
            seed_norms(3)
            y_norm(1)
            copy_M(2)
            y_norm(2)
            normalise3(0)
            copy_h2T(0)
            normalise3(1)
            y_norm(3)
            copy_h2T(1)
            gelu(0)
            y_norm(4)
            copy_M(3)
            gelu(1)
            normalise3(2)
            y_norm(5)
            copy_h2T(2)
            copy_s_row(0)
            normalise3(3)
            y_norm(6)
            copy_h2T(3)
            gelu(2)
            normalise3(4)
            copy_s_row(1)
            y_norm(7)
            gelu(3)
            copy_s_row(2)
            copy_h2T(4)
            normalise3(5)
            copy_s_row(3)
            copy_h2T(5)
            normalise3(6)
            copy_sums(0, 0)
            gelu(4)
            copy_sums(0, 1)
            copy_s_row(4)
            copy_h2T(6)
            gelu(5)
            copy_rank(0)
            copy_s_row(5)
            normalise3(7)
            copy_sums(1, 0)
            copy_h2T(7)
            gelu(6)
            copy_s_row(6)
            copy_sums(1, 1)
            gelu(7)
            copy_rank(1)
            copy_s_row(7)
            copy_sums(2, 0)
            copy_sums(2, 1)
            copy_rank(2)
            copy_sums(3, 0)
            copy_sums(3, 1)
            copy_rank(3)

        @block.vector
        def _(dve):
            chain = [0]

            def link(ins):
                chain[0] += 1
                ins.then_inc(dve_chain, 1)
                dve.wait_ge(dve_chain, chain[0])

            nc.vector.memset(ones3[:], 1.0)
            nc.vector.memset(minus1[:], -1.0).then_inc(dve_const, 1)

            nc.vector.memset(eps1[:], LN_EPS)
            nc.vector.memset(eps2[:, 0:TH], ATTN_EPS)
            link(nc.vector.memset(eps2[:, TH:T], LN_EPS))

            BIAS_STEPS = 6
            rstd_at = [0]
            RSTD_STEPS = 13

            def rstd(n, mean, m2, eps, v, y, t, i, r, shift):
                if n:
                    dve.wait_ge(rstd_step, rstd_at[0])
                if n == 0:
                    ins = nc.vector.scalar_tensor_tensor(out=v, in0=m2, scalar=1.0 / D, in1=eps, op0=ALU.mult, op1=ALU.add)
                elif n == 1:
                    ins = nc.vector.tensor_scalar(i, v.bitcast(I32), 1, None, ALU.logical_shift_right)
                elif n == 2:
                    ins = nc.vector.tensor_scalar(y.bitcast(I32), i, -1.0, float(0x5f3759df), ALU.mult, ALU.add)
                elif n == RSTD_STEPS - 1:
                    ins = nc.vector.scalar_tensor_tensor(out=shift, in0=mean, scalar=-1.0, in1=r, op0=ALU.mult, op1=ALU.mult)
                elif n % 3 == 0:
                    ins = nc.vector.tensor_tensor(t, y, y, ALU.mult)
                elif n % 3 == 1:
                    ins = nc.vector.scalar_tensor_tensor(out=t, in0=t, scalar=-0.5, in1=v, op0=ALU.mult, op1=ALU.mult)
                else:
                    ins = nc.vector.scalar_tensor_tensor(out=r if n == RSTD_STEPS - 2 else y, in0=t, scalar=1.5, in1=y,
                                                         op0=ALU.add, op1=ALU.mult)
                if n < RSTD_STEPS - 1:
                    rstd_at[0] += 1
                    ins.then_inc(rstd_step, 1)
                return ins

            def bn_x(b, g):
                if g % 2 == 0:
                    dve.wait_ge(x_in[2 * b + g // 2], 16)
                return nc.vector.bn_stats(bn1[:, b, g, :], pairs(x_sb, T // 2 * b + g))

            def rstd1(n, b0, b1):
                v = bn1[:, b0:b1].rearrange("p b g (e s) -> p b (g e) s", s=3)
                cols = (a[:, b0:b1] for a in (eps1, var1, root1, root1b, bits1, r1, shift1))
                return rstd(n, v[:, :, :, 1], v[:, :, :, 2], *cols)

            def bias_step(n):
                if n == 0:
                    dve.wait_ge(bias_in, 16 * 4)
                    dve.wait_ge(later_set, 1)
                else:
                    dve.wait_ge(dve_chain, chain[0])
                if n == 0:
                    ins = nc.vector.tensor_scalar(bias_f[:, 0:2 * P], bias_f[:, 0:2 * P], 1.0, None, ALU.add)
                elif n == 5:
                    nc.vector.tensor_copy(bias3[:], bias_f[:]).then_inc(bias_set, 1)
                    return
                elif n % 2:
                    ins = nc.vector.tensor_copy(bias_cut[:], bias_f[:])
                else:
                    ins = nc.vector.scalar_tensor_tensor(out=bias_f[:], in0=bias_cut[:],
                                                         scalar=minus_later[:, n // 2 - 1:n // 2], in1=bias_f[:],
                                                         op0=ALU.mult, op1=ALU.add)
                chain[0] += 1
                ins.then_inc(dve_chain, 1)

            def normalise1(b):
                dve.wait_ge(r1_done, min(b + 1, 3))
                mean, _ = stats(bn1, b)
                for t in range(TH):
                    last = nc.vector.tensor_scalar(norm_sb[:, T * b + t], x_sb[:, T * b + t], mean[:, t:t + 1],
                                                   r1[:, b, t:t + 1], ALU.subtract, ALU.mult)
                last.then_inc(h_done, 1)

            def q_half(u):
                dve.wait_ge(expq_done, u + 1)
                nc.vector.scalar_tensor_tensor(out=qT[:, u], in0=exp_q[:, u % 2], scalar=1.0,
                                               in1=bank[:, Q_BANK, :], op0=ALU.min, op1=ALU.max).then_inc(q_done, 1)

            def k_half(u):
                dve.wait_ge(expk_done, u + 1)
                if u >= KRING:
                    dve.wait_ge(vk_full, (u - KRING) // 2 + 1)
                nc.vector.scalar_tensor_tensor(out=k_sb[:, u % KRING],
                                               in0=exp_k[:, u % 2].rearrange("p (t d) -> p t d", d=D), scalar=1.0,
                                               in1=kv_ps(u)[:, :, 0:P], op0=ALU.min, op1=ALU.max).then_inc(k_done, 1)

            def key_norms(b):
                dve.wait_ge(seed_done, b + 1)
                if b:
                    dve.wait_ge(kn_done, b)
                r, n = k_seed[:, b % 2], k_ssq[:, b % 2]
                link(nc.vector.tensor_tensor(k_tmp[:], r, r, ALU.mult))
                link(nc.vector.scalar_tensor_tensor(out=k_tmp[:], in0=k_tmp[:], scalar=-0.5, in1=n, op0=ALU.mult, op1=ALU.mult))
                nc.vector.scalar_tensor_tensor(out=k_rnorm[:], in0=k_tmp[:], scalar=1.5, in1=r, op0=ALU.add,
                                               op1=ALU.mult).then_inc(rnorm_done, 1)
                dve.wait_ge(rnorm_done, b + 1)
                a = 2 * b % KRING
                k = k_sb[:, a:a + 2].rearrange("p u t (h e) -> p (u t h) e", e=DEPTH)
                nc.vector.tensor_tensor(k, k, k_rnorm[:].unsqueeze(2).to_broadcast([P, T * HEADS, DEPTH]),
                                        ALU.mult).then_inc(kn_done, 1)

            def mask_vk(b):
                if b == 0:
                    dve.wait_ge(mask_set, 1)
                dve.wait_ge(vk_full, b + 1)
                nc.vector.tensor_tensor(vk_sb[:, b % 2], t_bank(("M", b))[:, 0:P], head_mask[:], ALU.mult).then_inc(vk_done, 1)

            def row_stats(s):
                if s < U:
                    dve.wait_ge(y_full, s + 1)
                    y = bank[:, Y_BANKS[s], :].rearrange("p (t d) -> p t d", d=D)
                    for g in range(TH // 2):
                        last = nc.vector.bn_stats(bn2[:, s, g, :], pairs(y, g))
                if s >= XL:
                    u = s - XL
                    dve.wait_ge(x1_done, u + 1)
                    for g in range(TH // 2):
                        last = nc.vector.bn_stats(bn2[:, s, TH // 2 + g, :], pairs(x_sb, TH // 2 * u + g))
                link(last)
                now[:] = s, 0

            def rstd2(n, s):
                c0, c1 = 0 if s < U else TH, T if s >= XL else TH
                ins = rstd(n, *(a[:, c0:c1] for a in (*stats(bn2, s), eps2, var, root, root2, bits, r2[:, s], shift2[:, s])))
                if n == RSTD_STEPS - 1:
                    ins.then_inc(r2_done, 1)

            def score_cols(u):
                dve.wait_ge(z_full, u + 1)
                nc.vector.tensor_copy(s_col[:, TH * u:TH * u + TH].rearrange("p (a t) -> p a t", a=2),
                                      z_ps()[:, :, :, P]).then_inc(s_col_done, 1)

            def compare(b, n):
                kind, J, c0, c1 = (early + late)[n]
                s = b % 2
                s_J = s_col[:, T * b:T * (b + 1)]
                if kind == "equal":
                    half = 2 * b + c0 // HW
                    dve.wait_ge(t_frees[1], t_at["s", half] + 1)
                    if b >= 2 and c0 == 0:
                        dve.wait_ge(t_fulls[1], t_at["r", b - 2] + 1)
                    nc.vector.tensor_tensor(ties[:, s, J:J + TH], s_row[:, b, c0:c1].rearrange("p (t i) -> p t i", i=P),
                                            s_J[:, J:J + TH].unsqueeze(2).to_broadcast([P, TH, P]), ALU.is_equal).then_inc(equal_done, 1)
                    return
                last = nc.vector.tensor_scalar(beats[:, s, J, c0:c1], s_row[:, b, c0:c1], s_J[:, J:J + 1], None,
                                               ALU.is_le)
                if c0 >= HW and J in (TH - 1, T - 1):
                    last.then_inc(beats_done, 1)

            def merge(b):
                dve.wait_ge(t_frees[BANK_OF["r"]], t_at["r", b] + 1)
                nc.vector.scalar_tensor_tensor(out=dropped[:, b % 2], in0=rank_sb[:, b % 2, T:2 * T], scalar=KEEP - 0.5,
                                               in1=rank_sb[:, b % 2, 0:T], op0=ALU.add, op1=ALU.is_lt).then_inc(dropped_done, 1)
                dve.wait_ge(dropped_done, b + 1)
                dve.wait_ge(gelu_sums, 2 * b + 2)
                dve.wait_ge(norm_sums, 2 * b + 2)
                for u in (2 * b, 2 * b + 1):
                    nc.vector.copy_predicated(g_sb[:, TH * u:TH * u + TH],
                                              dropped[:, b % 2, TH * (u % 2):TH * (u % 2) + TH].unsqueeze(2).to_broadcast([P, TH, D]),
                                              norm_sb[:, TH * u:TH * u + TH]).then_inc(merged, 1)

            def rstd_early(b):
                mean, m2 = stats(bn1, b)
                v, y, t = var1[:, b], root1[:, b], root1b[:, b]
                nc.vector.scalar_tensor_tensor(out=v, in0=m2, scalar=1.0 / D, in1=eps1[:, b], op0=ALU.mult,
                                               op1=ALU.add).then_inc(var_done, 1)
                dve.wait_ge(root_done, b + 1)
                link(nc.vector.tensor_tensor(t, y, y, ALU.mult))
                link(nc.vector.scalar_tensor_tensor(out=t, in0=t, scalar=-0.5, in1=v, op0=ALU.mult, op1=ALU.mult))
                link(nc.vector.scalar_tensor_tensor(out=r1[:, b], in0=t, scalar=1.5, in1=y, op0=ALU.add, op1=ALU.mult))
                nc.vector.scalar_tensor_tensor(out=shift1[:, b], in0=mean, scalar=-1.0, in1=r1[:, b], op0=ALU.mult,
                                               op1=ALU.mult).then_inc(r1_done, 1)

            for g in range(T // 2):
                last = bn_x(0, g)
            link(last)
            rstd_early(0)
            normalise1(0)
            for n in range(BIAS_STEPS):
                if 0 < n < T // 2:
                    bn_x(1, n - 1)
                bias_step(n)
            last = bn_x(1, T // 2 - 1)
            link(last)
            rstd_early(1)
            normalise1(1)

            now = [None, RSTD_STEPS]
            compared = [0]

            def rest_of_x_stats():
                for b in range(2, B):
                    for g in range(T // 2):
                        last = bn_x(b, g)
                link(last)
                now[:] = None, 0

            def compare_next(count):
                for n in range(compared[0], compared[0] + count):
                    compare(n // PIECES, n % PIECES)
                compared[0] += count

            def advance(steps, comparisons):
                for n in range(steps):
                    if now[0] is None:
                        last = rstd1(now[1], 2, B)
                        if now[1] == RSTD_STEPS - 1:
                            last.then_inc(r1_done, 1)
                    else:
                        rstd2(now[1], now[0])
                    now[1] += 1
                    if n < comparisons:
                        compare_next(1)

            q_half(0)
            rest_of_x_stats()
            k_half(0)
            k_half(1)
            advance(13, 0)
            normalise1(2)
            q_half(1)
            k_half(2)
            key_norms(0)
            k_half(3)
            normalise1(3)
            q_half(2)
            mask_vk(0)
            q_half(3)
            k_half(4)
            q_half(4)
            k_half(5)
            row_stats(0)
            advance(7, 0)
            q_half(5)
            advance(5, 0)
            advance(1, 0)
            key_norms(1)
            q_half(6)
            k_half(6)
            k_half(7)
            key_norms(2)
            mask_vk(1)
            q_half(7)
            row_stats(1)
            advance(5, 0)
            advance(8, 0)
            row_stats(2)
            mask_vk(2)
            advance(9, 0)
            advance(1, 0)
            advance(3, 0)
            row_stats(3)
            advance(13, 0)
            row_stats(4)
            key_norms(3)
            advance(2, 0)
            score_cols(0)
            advance(10, 0)
            mask_vk(3)
            advance(1, 0)
            row_stats(5)
            advance(2, 0)
            score_cols(1)
            advance(11, 0)
            row_stats(6)
            advance(13, 0)
            row_stats(7)
            score_cols(2)
            advance(9, 0)
            compare_next(1)
            advance(4, 0)
            row_stats(8)
            score_cols(3)
            advance(13, 13)
            row_stats(9)
            advance(1, 1)
            score_cols(4)
            advance(5, 5)
            score_cols(5)
            advance(7, 6)
            compare_next(4)
            score_cols(6)
            compare_next(5)
            merge(0)
            score_cols(7)
            compare_next(4)
            compare_next(11)
            compare_next(6)
            merge(1)
            merge(2)
            merge(3)

        @block.tensor
        def _(pe):
            def take_t(use):
                if t_at[use] >= 1:
                    pe.wait_ge(t_frees[BANK_OF[use[0]]], t_at[use])

            def transpose_h(u):
                pe.wait_ge(h_done_act if u % 2 else h_done, u // 2 + 1)
                if u == 0:
                    pe.wait_ge(ident_set, 1)
                take_t(("h", u))
                for t in range(TH):
                    last = nc.tensor.transpose(t_bank(("h", u))[:, t * P:(t + 1) * P], norm_sb[:, TH * u + t], ident[:])
                last.then_inc(t_fulls[0], 1)

            def q_proj(u):
                pe.wait_ge(t_frees[BANK_OF["h"]], t_at["h", u] + 1)
                if u == 0:
                    pe.wait_ge(wq_in, 16)
                if u >= 1:
                    pe.wait_ge(q_done, u)
                o = bank[:, Q_BANK, :]
                nc.tensor.matmul(o, wq_sb[:], hT[:, u], start=True, stop=False)
                if u == 0:
                    pe.wait_ge(bias_set, 1)
                    pe.wait_ge(dve_const, 1)
                nc.tensor.matmul(o, bias3[:, 0:P], ones3[:], start=False, stop=True).then_inc(q_full, 1)

            def kv_proj(u):
                pe.wait_ge(t_frees[BANK_OF["h"]], t_at["h", u] + 1)
                if u == 0:
                    pe.wait_ge(wkv_in, 32)
                    pe.wait_ge(bias_set, 1)
                    pe.wait_ge(dve_const, 1)
                if u >= 2:
                    pe.wait_ge(v_done, u - 1)
                for t in range(TH):
                    o = kv_ps(u)[:, t, :]
                    nc.tensor.matmul(o, hT[:, u, t * P:(t + 1) * P], wkv_sb[:], start=True, stop=False)
                    last = nc.tensor.matmul(o, ones3[:, 0:P], bias3[:, P:3 * P], start=False, stop=True)
                last.then_inc(kv_full, 1)

            def attention_matrix(b):
                pe.wait_ge(kn_done, b + 1)
                pe.wait_ge(v_done, 2 * b + 2)
                take_t(("M", b))
                o = t_bank(("M", b))
                for t in range(T):
                    u = 2 * b + t // TH
                    last = nc.tensor.matmul(o[:, 0:P], v_sb[:, u % KRING, t % TH], k_sb[:, u % KRING, t % TH], start=(t == 0), stop=(t == T - 1))
                last.then_inc(vk_full, 1)

            def attention_out(b):
                if b == 0:
                    pe.wait_ge(wo_in, 16)
                pe.wait_ge(vk_done, b + 1)
                nc.tensor.matmul(t_bank(("M", b))[:, P:2 * P], vk_sb[:, b % 2], wo_sb[:], start=True, stop=True).then_inc(t_fulls[1], 1)

            def y_half(u):
                b = u // 2
                pe.wait_ge(t_frees[BANK_OF["M"]], t_at["M", b] + 1)
                pe.wait_ge(q_done, u + 1)
                earlier = [w for w in range(u) if Y_BANKS[w] == Y_BANKS[u]]
                if earlier:
                    pe.wait_ge(yn_done, earlier[-1] + 1)
                elif Y_BANKS[u] == Q_BANK:
                    pe.wait_ge(q_done, U)
                elif Y_BANKS[u] in (4, 5):
                    pe.wait_ge(v_done, U)
                for t in range(TH):
                    o = bank[:, Y_BANKS[u], t * P:(t + 1) * P]
                    nc.tensor.matmul(o, qT[:, u, t * P:(t + 1) * P], M_sb[:, b], start=True, stop=False)
                    nc.tensor.matmul(o, hT[:, u, t * P:(t + 1) * P], ident[:], start=False, stop=False)
                    last = nc.tensor.matmul(o, ones3[:, 0:P], bias3[:, 3 * P:4 * P], start=False, stop=True)
                last.then_inc(y_full, 1)

            def transpose_h2(u):
                pe.wait_ge(h2_done, u + 1)
                take_t(("h2", u))
                for t in range(TH):
                    last = nc.tensor.transpose(t_bank(("h2", u))[:, t * P:(t + 1) * P], norm_sb[:, TH * u + t], ident[:])
                last.then_inc(t_fulls[0], 1)

            def z_half(u):
                pe.wait_ge(t_frees[BANK_OF["h2"]], t_at["h2", u] + 1)
                if u == 0:
                    pe.wait_ge(wz_in, 32)
                    pe.wait_ge(v_done, U)
                if u >= 1:
                    pe.wait_ge(gelu_done, u)
                    pe.wait_ge(s_col_done, u)
                for t in range(TH):
                    last = nc.tensor.matmul(z_ps()[:, t // 2, t % 2, :], h2T[:, u % 2, t * P:(t + 1) * P], wz_sb[:],
                                            start=True, stop=True)
                last.then_inc(z_full, 1)

            def score_rows(u):
                pe.wait_ge(s_col_done, u + 1)
                take_t(("s", u))
                for t in range(TH):
                    n = TH * u + t
                    last = nc.tensor.transpose(t_bank(("s", u))[:, t * P:(t + 1) * P],
                                               s_col[:, n:n + 1].to_broadcast([P, P]), ident[:])
                last.then_inc(t_fulls[1], 1)

            def row_sums(b, half):
                s, use = b % 2, ("ta", "tb")[half]
                if b == 0:
                    pe.wait_ge(mask_set, 1)
                pe.wait_ge(beats_done, 2 * b + half + 1)
                take_t((use, b))
                o = t_bank((use, b))
                for n in range(TH):
                    J = TH * half + n
                    for I in range(J, T):
                        last = nc.tensor.matmul(o[:, n * P:(n + 1) * P], beats[:, s, J, I * P:(I + 1) * P], ident16[:],
                                                start=(I == J), stop=(I == T - 1))
                last.then_inc(t_fulls[BANK_OF[use]], 1)

            def rank(b):
                s = b % 2
                pe.wait_ge(beats_done, 2 * b + 2)
                pe.wait_ge(ties_done, 2 * b + 2)
                take_t(("r", b))
                o = t_bank(("r", b))
                for i in range(T):
                    nc.tensor.matmul(o[:, i:i + 1], ones16[:], later_tiles[:, i:i + 1], start=True, stop=False)
                    for J in range(i):
                        nc.tensor.matmul(o[:, i:i + 1], beats[:, s, J, i * P:(i + 1) * P], ones16[:, 0:1],
                                         start=False, stop=False)
                    nc.tensor.matmul(o[:, i:i + 1], ties[:, s, i], ones16[:, 0:1], start=False, stop=True)
                pe.wait_ge(t_frees[0], t_at["tb", b] + 1)
                pe.wait_ge(t_frees[1], t_at["ta", b] + 1)
                for J in range(T):
                    last = nc.tensor.matmul(o[:, T + J:T + J + 1], part_sums[:, J * P:(J + 1) * P], ones16[:, 0:1],
                                            start=True, stop=True)
                last.then_inc(t_fulls[1], 1)

            transpose_h(0)
            q_proj(0)
            transpose_h(1)
            kv_proj(0)
            transpose_h(2)
            kv_proj(1)
            q_proj(1)
            transpose_h(3)
            kv_proj(2)
            kv_proj(3)
            transpose_h(4)
            q_proj(2)
            transpose_h(5)
            kv_proj(4)
            attention_matrix(0)
            q_proj(3)
            attention_out(0)
            transpose_h(6)
            kv_proj(5)
            q_proj(4)
            y_half(0)
            q_proj(5)
            kv_proj(6)
            transpose_h(7)
            q_proj(6)
            kv_proj(7)
            attention_matrix(1)
            q_proj(7)
            y_half(1)
            attention_out(1)
            y_half(2)
            attention_matrix(2)
            attention_out(2)
            y_half(3)
            y_half(4)
            transpose_h2(0)
            y_half(5)
            transpose_h2(1)
            z_half(0)
            attention_matrix(3)
            z_half(1)
            attention_out(3)
            y_half(6)
            score_rows(0)
            transpose_h2(2)
            y_half(7)
            z_half(2)
            score_rows(1)
            transpose_h2(3)
            z_half(3)
            score_rows(2)
            transpose_h2(4)
            score_rows(3)
            z_half(4)
            transpose_h2(5)
            row_sums(0, 0)
            row_sums(0, 1)
            score_rows(4)
            z_half(5)
            transpose_h2(6)
            rank(0)
            score_rows(5)
            z_half(6)
            row_sums(1, 0)
            transpose_h2(7)
            score_rows(6)
            row_sums(1, 1)
            z_half(7)
            rank(1)
            score_rows(7)
            row_sums(2, 0)
            row_sums(2, 1)
            rank(2)
            row_sums(3, 0)
            row_sums(3, 1)
            rank(3)


_INS = ['L0_attn_x', 'L0_attn_Wq', 'L0_attn_bq', 'L0_attn_Wk', 'L0_attn_bk', 'L0_attn_Wv', 'L0_attn_bv', 'L0_attn_Wo',
        'L0_attn_bo', 'L0_attn_gamma', 'L0_attn_beta', 'L0_ffn_w_router', 'L0_ffn_w_block']
_OUTS = [((4, 1024, 128), 'float32')]


def kernel(**inputs):
    import numpy as _np
    import concourse.bacc as _bacc
    from concourse import mybir as _mybir
    from concourse.bass_utils import run_bass_kernel_spmd as _run

    nc = _bacc.Bacc("TRN2", target_bir_lowering=False, num_devices=1)
    arrays, args = {}, []
    for name in _INS:
        a = _np.ascontiguousarray(inputs[name])
        arrays[f"in_{name}_dram"] = a
        args.append(nc.dram_tensor(f"in_{name}_dram", a.shape, _mybir.dt.from_np(a.dtype), kind="ExternalInput").ap())
    for i, (shape, dtype) in enumerate(_OUTS):
        dt = _mybir.dt.from_np(_np.dtype(dtype))
        args.append(nc.dram_tensor(f"out_{i}_dram", shape, dt, kind="ExternalOutput").ap())
    preln_linear_attention_mod_ffn(nc, *args)
    r = _run(nc, [arrays], core_ids=[0])
    got = tuple(r.results[0][f"out_{i}_dram"] for i in range(len(_OUTS)))
    return got[0]
```
